# Optimizing a Trainium2 kernel written in Bass

```python
import numpy as np
import jax
import jax.numpy as jnp

def _softmax(x, axis=-1):
    return jax.nn.softmax(x, axis=axis)

def _gelu(x):
    return jax.nn.gelu(x, approximate=True)

def _silu(x):
    return jax.nn.silu(x)

def _sigmoid(x):
    return jax.nn.sigmoid(x)

def _layernorm(x, axis=-1, eps=1e-05):
    m = jnp.mean(x, axis=axis, keepdims=True)
    v = jnp.var(x, axis=axis, keepdims=True)
    return (x - m) / jnp.sqrt(v + eps)

def _scatter_add(tgt, idx, src, axis=0):
    return tgt.at[idx].add(src)

def _segment_sum(src, seg, n):
    return jax.ops.segment_sum(src, seg, n)
kernel_name = 'mk_adaln_d1_jaxref_r8_d29ed9'

def setup_inputs(seed: int=0):
    np.random.seed(seed)
    _w = jnp.asarray

    def _L0_attn_setup():
        import jax, jax.numpy as jnp
        import numpy as np
        key = jax.random.key(seed)
        ks = jax.random.split(key, 7)
        B, P, D = (4, 256, 128)
        s = 1.0 / np.sqrt(D)
        return {'x': jax.random.normal(ks[0], (B, P, D), dtype=jnp.float32), 'Wq': jax.random.normal(ks[1], (D, D), dtype=jnp.float32) * s, 'bq': jnp.zeros((D,), dtype=jnp.float32), 'Wk': jax.random.normal(ks[2], (D, D), dtype=jnp.float32) * s, 'bk': jnp.zeros((D,), dtype=jnp.float32), 'Wv': jax.random.normal(ks[3], (D, D), dtype=jnp.float32) * s, 'bv': jnp.zeros((D,), dtype=jnp.float32)}
    _L0_attn_in = _L0_attn_setup()

    def _L0_ffn_setup():
        import jax, jax.numpy as jnp
        import numpy as np
        import math
        BETA = 0.9
        THRESHOLD = 1.0
        NUM_STEPS = 5
        ALPHA = 2.0

        @jax.custom_vjp
        def spike_fn(u):
            return (u > 0).astype(u.dtype)

        def _spike_fwd(u):
            return (spike_fn(u), u)

        def _spike_bwd(u, g):
            s = jnp.pi / 2.0 * ALPHA * u
            return (g * (ALPHA / 2.0) / (1.0 + s * s),)
        spike_fn.defvjp(_spike_fwd, _spike_bwd)
        key = jax.random.key(seed)
        k1, k2, k3 = jax.random.split(key, 3)
        n_embd = 128
        x = jax.random.normal(k1, (4, 256, n_embd), dtype=jnp.float32)
        W_fc = jax.random.normal(k2, (4 * n_embd, n_embd), dtype=jnp.float32) / math.sqrt(n_embd)
        W_proj = jax.random.normal(k3, (n_embd, 4 * n_embd), dtype=jnp.float32) / math.sqrt(4 * n_embd)
        return {'x': x, 'W_fc': W_fc, 'W_proj': W_proj}
    _L0_ffn_in = _L0_ffn_setup()
    _L0_c = _w((lambda *s: np.random.randn(*s).astype(np.float32) * 0.05)(8, 128))
    _L0_wmod = _w((lambda *s: np.random.randn(*s).astype(np.float32) * 0.05)(128, 6 * 128) * 128 ** (-0.5))
    _d = {'L0_attn_x': _L0_attn_in['x'], 'L0_attn_Wq': _L0_attn_in['Wq'], 'L0_attn_bq': _L0_attn_in['bq'], 'L0_attn_Wk': _L0_attn_in['Wk'], 'L0_attn_bk': _L0_attn_in['bk'], 'L0_attn_Wv': _L0_attn_in['Wv'], 'L0_attn_bv': _L0_attn_in['bv'], 'L0_ffn_W_fc': _L0_ffn_in['W_fc'], 'L0_ffn_W_proj': _L0_ffn_in['W_proj'], 'L0_c': _L0_c, 'L0_wmod': _L0_wmod}
    _x0 = _d['L0_attn_x']
    _d['L0_attn_x'] = jax.random.normal(jax.random.fold_in(jax.random.key(seed), 1), (8, 1024, 128), dtype=_x0.dtype)
    del _x0
    return _d

def reference(L0_attn_x, L0_attn_Wq, L0_attn_bq, L0_attn_Wk, L0_attn_bk, L0_attn_Wv, L0_attn_bv, L0_ffn_W_fc, L0_ffn_W_proj, L0_c, L0_wmod):

    def _L0_attn_ref(x, Wq, bq, Wk, bk, Wv, bv):
        import jax, jax.numpy as jnp
        import numpy as np
        b, p, d = x.shape
        q = jnp.einsum('bpd,ed->bpe', x, Wq) + bq
        k = jnp.einsum('bpd,ed->bpe', x, Wk) + bk
        v = jnp.einsum('bpd,ed->bpe', x, Wv) + bv
        attn = jnp.einsum('bqd,bkd->bqk', q, k)
        causal = jnp.triu(jnp.ones((p, p), dtype=bool), k=1)
        attn = jnp.where(causal, -jnp.inf, attn)
        attn = attn / jnp.sqrt(jnp.asarray(d, dtype=attn.dtype))
        scores = jax.nn.softmax(attn, axis=-1)
        return jnp.einsum('bqk,bkd->bqd', scores, v)

    def _L0_ffn_ref(x, W_fc, W_proj):
        import jax, jax.numpy as jnp
        import numpy as np
        import math
        BETA = 0.9
        THRESHOLD = 1.0
        NUM_STEPS = 5
        ALPHA = 2.0

        @jax.custom_vjp
        def spike_fn(u):
            return (u > 0).astype(u.dtype)

        def _spike_fwd(u):
            return (spike_fn(u), u)

        def _spike_bwd(u, g):
            s = jnp.pi / 2.0 * ALPHA * u
            return (g * (ALPHA / 2.0) / (1.0 + s * s),)
        spike_fn.defvjp(_spike_fwd, _spike_bwd)
        h = jnp.square(jax.nn.relu(jnp.einsum('bsd,fd->bsf', x, W_fc)))
        y = jnp.einsum('bsf,df->bsd', h, W_proj)

        def step(mem, _):
            reset = jax.lax.stop_gradient(spike_fn(mem - THRESHOLD))
            mem_new = BETA * mem + y - reset * THRESHOLD
            spk = spike_fn(mem_new - THRESHOLD)
            return (mem_new, spk)
        mem0 = jnp.zeros_like(y)
        _, spks = jax.lax.scan(step, mem0, None, length=NUM_STEPS)
        return jnp.sum(spks, axis=0) / NUM_STEPS
    x = L0_attn_x
    mod = (_silu(L0_c) @ L0_wmod).reshape(L0_c.shape[0], 6, 1, -1)
    sa, ca, ga, sb, cb, gb = (mod[:, 0], mod[:, 1], mod[:, 2], mod[:, 3], mod[:, 4], mod[:, 5])
    ga = (2 * (ga >= 0) - 1) * jnp.maximum(jnp.abs(ga), 0.25)
    gb = (2 * (gb >= 0) - 1) * jnp.maximum(jnp.abs(gb), 0.25)
    h = _layernorm(x, axis=-1) * (1 + ca) + sa
    x = x + ga * _L0_attn_ref(h, L0_attn_Wq, L0_attn_bq, L0_attn_Wk, L0_attn_bk, L0_attn_Wv, L0_attn_bv)
    h = _layernorm(x, axis=-1) * (1 + cb) + sb
    x = x + gb * _L0_ffn_ref(h, L0_ffn_W_fc, L0_ffn_W_proj)
    return x

_drawn_inputs = setup_inputs


def setup_inputs(seed=0):
    import zlib

    import numpy as np

    out = dict(_drawn_inputs(seed))
    spreads = {'L0_attn_bq': (0.0, 2.0), 'L0_attn_bk': (0.0, 2.0), 'L0_attn_bv': (0.0, 0.317)}
    factors = {}
    for name, (base, spread) in spreads.items():
        noise = np.random.default_rng([zlib.crc32(name.encode()), seed]).standard_normal(out[name].shape)
        drawn = base * np.exp(spread * noise) if base else spread * noise
        out[name] = jnp.asarray(drawn.astype(out[name].dtype))
    for name, factor in factors.items():
        out[name] = (out[name] * factor).astype(out[name].dtype)
    return out
```

```python
import numpy as np
import concourse.bass as bass
from concourse import mybir
from contextlib import ExitStack

F32 = mybir.dt.float32
F32R = mybir.dt.float32r
BF16 = mybir.dt.bfloat16
ALU = mybir.AluOpType
ACT = mybir.ActivationFunctionType
AX = mybir.AxisListType

BETA, THRESHOLD, NUM_STEPS = 0.9, 1.0, 5
LN_EPS = 1e-5
GATE_MIN = 0.25
MASKED = -1e38


def spike_thresholds():
    one = np.float32(1)

    def spikes(current):
        mem, count = np.float32(0), 0
        for _ in range(NUM_STEPS):
            reset = one if mem > np.float32(THRESHOLD) else np.float32(0)
            mem = np.float32(BETA) * mem + current - reset * np.float32(THRESHOLD)
            count += int(mem > np.float32(THRESHOLD))
        return count

    thetas = []
    for n in range(NUM_STEPS):
        below = int(np.float32(0).view(np.int32))
        above = int(np.float32(2).view(np.int32))
        while above - below > 1:
            mid = (below + above) // 2
            if spikes(np.int32(mid).view(np.float32)) > n:
                above = mid
            else:
                below = mid
        thetas.append(float(np.int32(below).view(np.float32)))
    return thetas


def build(nc, x, c_t, w_mod, wq_t, wk_t, wv_t, w_fc_t, w_proj_t, bq, bk, bv, out):
    B, T, D = x.shape
    P = 128
    assert D == P and T % 512 == 0
    NT = T // P
    G = 4
    NG = NT // G
    W = G * P
    F = w_fc_t.shape[1]
    NF = F // P
    SHIFTA, SCALEA, GATEA, SHIFTB, SCALEB, GATEB = range(6)
    QK_SCALE = float(D) ** -0.5
    thetas = spike_thresholds()

    x_v = x.rearrange("b (t p) d -> b p t d", p=P)
    out_v = out.rearrange("b (t p) d -> b p t d", p=P)

    def pt_slots(t):
        return [("PT", t, h) for h in range(t // G + 1)]

    WORK_ORDER = [("QK", "q", 0), ("QK", "k", 0), ("QK", "q", 1), ("QK", "k", 1),
                  ("T2", 0), ("T2", 1)]
    for t in range(NT):
        WORK_ORDER += [*pt_slots(t), ("FC", t // NF, t % NF)]
        if t == 6:
            WORK_ORDER += [("OT", 0), ("O", 0)]
    WORK_ORDER += [("T1", 0), ("T1", 1), ("OT", 1), ("O", 1)]
    FFN_KINDS = ("T2", "FC", "OT")
    ATTENTION_ONLY = [s for s in WORK_ORDER if s[0] not in FFN_KINDS]
    FFN_ONLY = [s for s in WORK_ORDER if s[0] in FFN_KINDS]
    assert len(WORK_ORDER) % 2 == 0 and len(ATTENTION_ONLY) % 2 == 0 and NG % 2 == 0
    PT_NO = {}
    for t in range(NT):
        for step in pt_slots(t):
            PT_NO[step[1:]] = len(PT_NO)
    N_PT = len(PT_NO)
    N_PREP = 28

    def at(b, n):
        return isinstance(b, int) and b == n

    def order_of(b):
        return ATTENTION_ONLY if at(b, 0) else FFN_ONLY if at(b, B) else WORK_ORDER

    def place(b, step):
        i = order_of(b).index(step)
        before = NG
        if not at(b, 0):
            before = b * len(WORK_ORDER) + (NG + len(ATTENTION_ONLY) - len(WORK_ORDER))
        return before + i + 1, i % 2

    ctx = ExitStack()
    with ctx:
        def sb(name, shape, dt=F32):
            return ctx.enter_context(nc.sbuf_tensor(name, shape, dt))

        def pb(name, shape):
            return ctx.enter_context(nc.psum_tensor(name, shape, F32))

        def sem(name):
            return ctx.enter_context(nc.semaphore(name))

        ident = sb("ident", [P, P])
        ident16 = sb("ident16", [P, P], BF16)
        mask16 = sb("mask16", [P, P], BF16)
        ones = sb("ones", [1, P])
        minus_half = sb("minus_half", [P, G])
        ct_sb = sb("ct_sb", [P, B])
        silu_den = sb("silu_den", [P, B])
        silu_rec = sb("silu_rec", [P, B])
        silu = sb("silu", [P, B])
        wmod_sb = sb("wmod_sb", [P, 6 * D])
        wq_sb = sb("wq_sb", [P, D])
        wk_sb = sb("wk_sb", [P, D])
        wv_sb = sb("wv_sb", [P, D])
        wfc_sb = sb("wfc_sb", [P, F])
        wproj_sb = sb("wproj_sb", [P, NF, D])
        bq_sb = sb("bq_sb", [P, 1])
        bk_sb = sb("bk_sb", [P, 1])
        bv_sb = sb("bv_sb", [1, D])
        wq_s = sb("wq_s", [P, D])
        bq_s = sb("bq_s", [P, 1])
        wq_h, wq_l = sb("wq_h", [P, D], F32R), sb("wq_l", [P, D], F32R)
        wk_h, wk_l = sb("wk_h", [P, D], F32R), sb("wk_l", [P, D], F32R)
        wfc_h, wfc_l = sb("wfc_h", [P, F], F32R), sb("wfc_l", [P, F], F32R)
        mod = sb("mod", [P, 5, B + 1])
        CA, SA, CB, SB, GB = range(5)
        gate_sign = sb("gate_sign", [P, B * D])
        gate_size = sb("gate_size", [P, B * D])
        ga_rows = sb("ga_rows", [P, B, D])
        bcast = sb("bcast", [P, B, P])
        bcast2 = sb("bcast2", [P, B, P])
        wv_scaled = sb("wv_scaled", [P, B, D])
        wv_out = sb("wv_out", [P, B, D])
        bias_rows = sb("bias_rows", [P, B, D])
        gb_sign = sb("gb_sign", [P, B])
        gb_size = sb("gb_size", [P, B])

        x_in = sb("x_in", [P, NT, D])
        x_res = sb("x_res", [P, NT, D])
        z1 = sb("z1", [P, NT, D])
        z1_h, z1_l = sb("z1_h", [P, NT, D], F32R), sb("z1_l", [P, NT, D], F32R)
        h1 = sb("h1", [P, T])
        h1_h, h1_l = sb("h1_h", [P, T], F32R), sb("h1_l", [P, T], F32R)
        q_h, q_l = sb("q_h", [P, T], F32R), sb("q_l", [P, T], F32R)
        k_h, k_l = sb("k_h", [P, T], F32R), sb("k_l", [P, T], F32R)
        probs = sb("probs", [P, 2, T])
        NS = NT
        p_h, p_l = sb("p_h", [P, NS, W], F32R), sb("p_l", [P, NS, W], F32R)
        attended = sb("attended", [P, NG, W])
        x1 = sb("x1", [P, NT, D])
        z2 = sb("z2", [P, NT, D])
        h2 = sb("h2", [P, T])
        h2_h, h2_l = sb("h2_h", [P, T], F32R), sb("h2_l", [P, T], F32R)
        relu = sb("relu", [P, 2, W])
        act2 = sb("act2", [P, 2, W])
        spikes = sb("spikes", [P, 2, W])
        spikes_g = sb("spikes_g", [P, 2, W])
        y_out = sb("y_out", [P, NG, G, D])
        neg_max = sb("neg_max", [P, NT])
        row_sum = sb("row_sum", [P, NT])
        row_rec = sb("row_rec", [P, NT])
        stats1, stats2 = sb("stats1", [P, NT, 6]), sb("stats2", [P, NT, 6])
        mv1, mv2 = sb("mv1", [P, NT, 2]), sb("mv2", [P, NT, 2])
        var1, var2 = sb("var1", [P, NT]), sb("var2", [P, NT])
        rstd1, rstd2 = sb("rstd1", [P, NT]), sb("rstd2", [P, NT])

        scores = pb("scores", [P, 2, T])
        acc = pb("acc", [P, W])
        current = pb("current", [P, W])
        work = pb("work", [P, 2, W])

        c_loaded, w_loaded, x_loaded = sem("c_loaded"), sem("w_loaded"), sem("x_loaded")
        stored = [sem(f"stored{g}") for g in range(NG)]
        const_step = sem("const_step")
        silu_step = sem("silu_step")
        act_waited, dve_waited, pool_waited = sem("act_waited"), sem("dve_waited"), sem("pool_waited")
        prep = sem("prep")
        prep_mm = sem("prep_mm")
        work_ready = sem("work_ready")
        scores_ready = sem("scores_ready")
        acc_ready = sem("acc_ready")
        down_done = sem("down_done")
        qk_high, qk_low = sem("qk_high"), sem("qk_low")
        probs_ready = sem("probs_ready")
        pt_high, pt_low = sem("pt_high"), sem("pt_low")
        attended_ready = sem("attended_ready")
        h1_full, h1_high, h1_low = sem("h1_full"), sem("h1_high"), sem("h1_low")
        h2_full, h2_high, h2_low = sem("h2_full"), sem("h2_high"), sem("h2_low")
        relu_ready, act2_ready = sem("relu_ready"), sem("act2_ready")
        spike_step = sem("spike_step")
        spikes_scaled = sem("spikes_scaled")
        y_ready = sem("y_ready")
        max_ready = sem("max_ready")
        rec_ready = sem("rec_ready")
        x1_ready = sem("x1_ready")
        bn1, bn2 = sem("bn1"), sem("bn2")
        mv1_ready, mv2_ready = sem("mv1_ready"), sem("mv2_ready")
        rstd1_step, rstd2_step = sem("rstd1_step"), sem("rstd2_step")
        z1_ready, z2_ready = sem("z1_ready"), sem("z2_ready")
        z1_high, z1_low = sem("z1_high"), sem("z1_low")
        x_res_ready = sem("x_res_ready")

        block = ctx.enter_context(nc.Block())

        def cols(g):
            return slice(g * W, (g + 1) * W)

        def slot(g, kt):
            return kt + (NS - G * (g + 1))

        def plain(ap):
            return ap.bitcast(F32)

        @block.sync
        def _(sp):
            sp.dma_start(ct_sb[:, :], c_t).then_inc(c_loaded, 16)
            sp.dma_start(wmod_sb[:, :], w_mod).then_inc(c_loaded, 16)
            sp.dma_start(x_in[:, :, :], x_v[0]).then_inc(x_loaded, 16)
            for dst, src in ((wq_sb, wq_t), (wk_sb, wk_t), (wv_sb, wv_t), (wfc_sb, w_fc_t),
                             (bq_sb, bq), (bk_sb, bk), (bv_sb, bv)):
                sp.dma_start(dst[:, :], src).then_inc(w_loaded, 16)
            sp.dma_start(wproj_sb[:, :, :], w_proj_t).then_inc(w_loaded, 16)

            def next_x(b, src):
                sp.wait_ge(x_res_ready, NG * b + NG)
                sp.wait_ge(z1_ready, NT * b + NT)
                sp.dma_start(x_in[:, :, :], src).then_inc(x_loaded, 16)

            def store(f, g):
                sp.wait_ge(y_ready, NG * f + g + 1)
                sp.dma_start(out_v[f][:, g * G:(g + 1) * G, :], y_out[:, g, :, :]).then_inc(stored[g], 16)

            next_x(0, x_v[1])
            with sp.Fori(1, B - 1) as b:
                next_x(b, x_v[b + 1])
                for g in range(NG):
                    store(b - 1, g)
            next_x(B - 1, x_v[0])
            for f in (B - 2, B - 1):
                for g in range(NG):
                    store(f, g)
            for g in range(NG):
                sp.wait_ge(stored[g], 16 * B)
            sp.wait_ge(x_loaded, 16 * (B + 1))

        @block.tensor
        def _(pe):
            mm = nc.tensor.matmul

            def three(dst, a_h, a_l, b_h, b_l, start=True, stop=True):
                mm(dst, a_h, b_h, start=start, stop=False)
                mm(dst, a_l, b_h, start=False, stop=False)
                return mm(dst, a_h, b_l, start=False, stop=stop)

            pe.wait_ge(const_step, 7)
            pe.wait_ge(prep, 1)
            pe.wait_ge(c_loaded, 32)
            for n, j in enumerate((SCALEA, SHIFTA, SCALEB, SHIFTB, GATEB)):
                mm(scores[:, 0, n * B:(n + 1) * B], wmod_sb[:, j * D:(j + 1) * D], silu[:, :],
                   start=True, stop=True).then_inc(prep_mm, 1)
            pe.wait_ge(prep, 2)
            for b in range(B):
                mm(scores[:, 1, b * D:(b + 1) * D], bcast[:, b, :],
                   wmod_sb[:, GATEA * D:(GATEA + 1) * D], start=True, stop=True).then_inc(prep_mm, 1)
            pe.wait_ge(prep, 4)
            pe.wait_ge(w_loaded, 8 * 16)
            for b in range(B):
                dst = scores[:, 0, b * D:(b + 1) * D]
                mm(dst, bcast2[:, b, :], wv_sb[:, :], start=True, stop=False)
                mm(dst, ones[:, :], bv_sb[:, :], start=False, stop=True).then_inc(prep_mm, 1)

            def bank_reader(b, step):
                kind, rest = step[0], step[1:]
                if kind == "QK":
                    return qk_low, 2 * NG * b + 2 * rest[1] + (rest[0] == "k") + 1
                if kind == "PT":
                    return pt_low, N_PT * b + PT_NO[rest] + 1
                if kind == "T1":
                    return h1_full, NG * (b + 1) + rest[0] + 1
                if kind == "T2":
                    return h2_full, NG * (b - 1) + rest[0] + 1
                if kind == "FC":
                    return relu_ready, NG * NF * (b - 1) + NF * rest[0] + rest[1] + 1
                if kind == "O":
                    return x1_ready, NT * b + G * (rest[0] + 1)
                return y_ready, NG * (b - 1) + rest[0] + 1

            def work_tile(b, step):
                i = order_of(b).index(step)
                if i >= 2:
                    reader, count = bank_reader(b, order_of(b)[i - 2])
                elif at(b, 0):
                    reader, count = bank_reader(-1, ("T1", i))
                else:
                    last = ATTENTION_ONLY if at(b, 1) else WORK_ORDER
                    reader, count = bank_reader(b - 1, last[i - 2])
                pe.wait_ge(reader, count)
                return work[:, i % 2, :]

            def rows_to_columns(dst, src, g):
                for i in range(G):
                    last = nc.tensor.transpose(dst[:, i * P:(i + 1) * P], src[:, g * G + i, :], ident[:, :])
                return last

            def t1(n, g, dst):
                pe.wait_ge(z1_ready, NT * n + G * (g + 1))
                rows_to_columns(dst, z1, g).then_inc(work_ready, 1)

            for g in range(NG):
                t1(0, g, work[:, g, :])
            pe.wait_ge(prep, N_PREP)

            def qk(b, which, g):
                w_h, w_l = (wq_h, wq_l) if which == "q" else (wk_h, wk_l)
                dst = work_tile(b, ("QK", which, g))
                pe.wait_ge(h1_high, NG * b + g + 1)
                pe.wait_ge(h1_low, NG * b + g + 1)
                three(dst, w_h[:, :], w_l[:, :], h1_h[:, cols(g)], h1_l[:, cols(g)]).then_inc(work_ready, 1)

            def score(b, t):
                g = t // G
                pe.wait_ge(qk_low, 2 * NG * b + 2 * g + 2)
                if not (at(b, 0) and t < 2):
                    pe.wait_ge(probs_ready, NT * b + t - 1)
                width = (t + 1) * P
                rows = slice(t * P, (t + 1) * P)
                for lo in range(0, width, W):
                    n = max(min(width - lo, W), 2 * P)
                    diagonal = lo + W >= width
                    three(scores[:, t % 2, lo:lo + n], q_h[:, rows], q_l[:, rows],
                          k_h[:, lo:lo + n], k_l[:, lo:lo + n], stop=not diagonal)
                last = mm(scores[:, t % 2, t * P:width], ident16[:, :], mask16[:, :],
                          start=False, stop=True)
                last.then_inc(scores_ready, 1)

            def transpose_probs(b, t, h):
                dst = work_tile(b, ("PT", t, h))
                pe.wait_ge(probs_ready, NT * b + t + 1)
                blocks = range(h * G, min(h * G + G, t + 1))
                for kt in blocks:
                    last = nc.tensor.transpose(dst[:, (kt - h * G) * P:(kt - h * G + 1) * P],
                                               probs[:, t % 2, kt * P:(kt + 1) * P], ident[:, :])
                last.then_inc(work_ready, 1)

            def attend(b, g):
                pe.wait_ge(pt_low, N_PT * b + PT_NO[(G * g + G - 1, g)] + 1)
                pe.wait_ge(z1_low, NG * b + g + 1)
                if not (at(b, 0) and g == 0):
                    pe.wait_ge(attended_ready, NG * b + g)
                last_kt = G * (g + 1) - 1
                for kt in range(last_kt + 1):
                    c0 = min(max(kt - G * g, 0) * P, W - 2 * P)
                    s = slot(g, kt)
                    last = three(acc[:, c0:W], z1_h[:, kt, :], z1_l[:, kt, :],
                                 p_h[:, s, c0:W], p_l[:, s, c0:W], start=kt == 0, stop=kt == last_kt)
                last.then_inc(acc_ready, 1)

            def project_out(b, g):
                dst = work_tile(b, ("O", g))
                pe.wait_ge(attended_ready, NG * b + g + 1)
                for i in range(G):
                    last = mm(dst[:, i * P:(i + 1) * P], attended[:, g, i * P:(i + 1) * P],
                              wv_out[:, b, :], start=True, stop=True)
                last.then_inc(work_ready, 1)

            def t2(b, g):
                dst = work_tile(b, ("T2", g))
                pe.wait_ge(z2_ready, NT * (b - 1) + G * (g + 1))
                rows_to_columns(dst, z2, g).then_inc(work_ready, 1)

            def up(b, c, j):
                dst = work_tile(b, ("FC", c, j))
                pe.wait_ge(h2_high, NG * (b - 1) + c + 1)
                pe.wait_ge(h2_low, NG * (b - 1) + c + 1)
                w = slice(j * P, (j + 1) * P)
                three(dst, wfc_h[:, w], wfc_l[:, w], h2_h[:, cols(c)], h2_l[:, cols(c)])\
                    .then_inc(work_ready, 1)

            def down(b, c, j):
                f = b - 1
                pe.wait_ge(act2_ready, NG * NF * f + NF * c + j + 1)
                if j == 0 and not (at(b, 1) and c == 0):
                    pe.wait_ge(spike_step, NUM_STEPS * (NG * f + c))
                mm(current[:, :], wproj_sb[:, j, :], act2[:, j % 2, :],
                   start=j == 0, stop=j == NF - 1).then_inc(down_done, 1)

            def spikes_back(b, c):
                dst = work_tile(b, ("OT", c))
                pe.wait_ge(spikes_scaled, NG * (b - 1) + c + 1)
                for i in range(G):
                    last = nc.tensor.transpose(dst[:, i * P:(i + 1) * P],
                                               spikes_g[:, c, i * P:(i + 1) * P], ident[:, :])
                last.then_inc(work_ready, 1)

            def iteration(b, ffn=True, attention=True):
                if attention:
                    for g in range(NG):
                        qk(b, "q", g)
                        qk(b, "k", g)
                    score(b, 0)
                    score(b, 1)
                if ffn:
                    for g in range(NG):
                        t2(b, g)
                for t in range(NT):
                    c, j = divmod(t, NF)
                    if attention:
                        for _, _, h in pt_slots(t):
                            transpose_probs(b, t, h)
                        if t + 2 < NT:
                            score(b, t + 2)
                    if ffn:
                        up(b, c, j)
                        if j > 0:
                            down(b, c, j - 1)
                        if t == 6:
                            spikes_back(b, 0)
                    if attention and t == 6:
                        project_out(b, 0)
                    if attention and t == G - 1:
                        attend(b, 0)
                    if ffn and t == NF - 1:
                        down(b, 0, NF - 1)
                if attention:
                    for g in range(NG):
                        t1(b + 1, g, work_tile(b, ("T1", g)))
                if ffn:
                    down(b, 1, NF - 1)
                if attention:
                    attend(b, 1)
                if ffn:
                    spikes_back(b, 1)
                if attention:
                    project_out(b, 1)

            iteration(0, ffn=False)
            iteration(1)
            with pe.Fori(2, B) as b:
                iteration(b)
            iteration(B, attention=False)

        @block.scalar
        def _(act):
            act.wait_ge(c_loaded, 32)
            nc.scalar.activation(silu_den[:, :], ct_sb[:, :], ACT.Exp, scale=-1.0).then_inc(silu_step, 1)

            def ready(b, step):
                count, bank = place(b, step)
                act.wait_ge(work_ready, count)
                return work[:, bank, :]

            def waited():
                act.sem_inc(act_waited, 1)

            def qk_h(b, which, g):
                src = ready(b, ("QK", which, g))
                if g == 0 and which == "q" and not at(b, 0):
                    act.wait_ge(scores_ready, NT * b)
                dst, bias = (q_h, bq_s) if which == "q" else (k_h, bk_sb)
                nc.scalar.activation(dst[:, cols(g)], src, ACT.Identity, bias=bias[:, 0:1]).then_inc(qk_high, 1)

            def exponential(b, t):
                n = NT * b + t
                act.wait_ge(max_ready, n + 1)
                if t >= 2:
                    act.wait_ge(work_ready, place(b, pt_slots(t - 2)[-1])[0])
                elif not at(b, 0):
                    act.wait_ge(rec_ready, NG * b)
                width = (t + 1) * P
                nc.scalar.activation(probs[:, t % 2, 0:width], scores[:, t % 2, 0:width], ACT.Exp,
                                     bias=neg_max[:, t:t + 1],
                                     accum_out=row_sum[:, t:t + 1]).then_inc(probs_ready, 1)

            def pt_h(b, t, h):
                src = ready(b, ("PT", t, h))
                g, n = t // G, min(G, t + 1 - h * G)
                if t % G == 0 and h == 0 and not (at(b, 0) and g == 0):
                    act.wait_ge(acc_ready, NG * b + g)
                s = slot(g, h * G)
                nc.scalar.activation(p_h[:, s:s + n, (t % G) * P:(t % G + 1) * P],
                                     src[:, 0:n * P].rearrange("p (k q) -> p k q", q=P),
                                     ACT.Copy).then_inc(pt_high, 1)

            def copy_attended(b, g):
                act.wait_ge(acc_ready, NG * b + g + 1)
                nc.scalar.activation(attended[:, g, :], acc[:, :], ACT.Copy).then_inc(attended_ready, 1)

            def modulate1(n, src, g):
                waited()
                nc.scalar.activation(h1[:, cols(g)], src, ACT.Identity, bias=mod[:, SA, bass.ds(n, 1)],
                                     scale=mod[:, CA, bass.ds(n, 1)]).then_inc(h1_full, 1)

            def modulate2(b, g):
                src = ready(b, ("T2", g))
                if not at(b, 1):
                    act.wait_ge(h2_low, NG * (b - 2) + g + 1)
                f = b - 1
                waited()
                nc.scalar.activation(h2[:, cols(g)], src, ACT.Identity, bias=mod[:, SB, bass.ds(f, 1)],
                                     scale=mod[:, CB, bass.ds(f, 1)]).then_inc(h2_full, 1)

            def rectify(b, c, j):
                src = ready(b, ("FC", c, j))
                n = NG * NF * (b - 1) + NF * c + j
                if not (at(b, 1) and c == 0 and j < 2):
                    act.wait_ge(act2_ready, n - 1)
                nc.scalar.activation(relu[:, j % 2, :], src, ACT.Relu).then_inc(relu_ready, 1)

            def scale_spikes(b, c):
                f = b - 1
                act.wait_ge(spike_step, NUM_STEPS * (NG * f + c + 1))
                waited()
                nc.scalar.activation(spikes_g[:, c, :], spikes[:, c, :], ACT.Identity,
                                     scale=mod[:, GB, bass.ds(f, 1)]).then_inc(spikes_scaled, 1)

            act.wait_ge(prep, N_PREP)
            for g in range(NG):
                act.wait_ge(work_ready, g + 1)
                modulate1(0, work[:, g, :], g)

            def iteration(b, ffn=True, attention=True):
                if attention:
                    for g in range(NG):
                        qk_h(b, "q", g)
                        qk_h(b, "k", g)
                    exponential(b, 0)
                if ffn:
                    for g in range(NG):
                        modulate2(b, g)
                if attention:
                    exponential(b, 1)
                for t in range(NT):
                    c, j = divmod(t, NF)
                    if attention:
                        for step in pt_slots(t):
                            pt_h(b, *step[1:])
                    if ffn:
                        rectify(b, c, j)
                    if ffn and t == NF + 1:
                        scale_spikes(b, 0)
                    if attention:
                        if t + 2 < NT:
                            exponential(b, t + 2)
                        if t == G - 1:
                            copy_attended(b, 0)
                if attention:
                    for g in range(NG):
                        src = ready(b, ("T1", g))
                        act.wait_ge(h1_low, NG * b + g + 1)
                        modulate1(b + 1, src, g)
                    copy_attended(b, 1)
                if ffn:
                    scale_spikes(b, 1)

            iteration(0, ffn=False)
            iteration(1)
            with act.Fori(2, B) as b:
                iteration(b)
            iteration(B, attention=False)

        @block.vector
        def _(dve):
            v = nc.vector
            def waited():
                dve.sem_inc(dve_waited, 1)

            def statistics(src, stats, mv, counted, ready_, n, g):
                for i in range(G * g, G * g + G):
                    v.bn_stats(stats[:, i, :], src[:, i, :]).then_inc(counted, 1)
                dve.wait_ge(counted, NT * n + G * (g + 1))
                waited()
                for i in range(G * g, G * g + G):
                    v.bn_aggr(mv[:, i, :], stats[:, i, :]).then_inc(ready_, 1)

            def statistics1(n, g):
                if g == 0:
                    dve.wait_ge(x_loaded, 16 * (n + 1))
                    if not at(n, 0):
                        dve.wait_ge(z1_ready, NT * n)
                statistics(x_in, stats1, mv1, bn1, mv1_ready, n, g)

            def work_bank(b, step):
                return work[:, place(b, step)[1], :]

            def qk_l(b, which, g):
                n = 2 * NG * b + 2 * g + (which == "k")
                dve.wait_ge(qk_high, n + 1)
                high, low, bias = (q_h, q_l, bq_s) if which == "q" else (k_h, k_l, bk_sb)
                v.scalar_tensor_tensor(low[:, cols(g)], work_bank(b, ("QK", which, g)), bias[:, 0:1],
                                       plain(high[:, cols(g)]), ALU.add, ALU.subtract).then_inc(qk_low, 1)

            def maximum(b, t):
                dve.wait_ge(scores_ready, NT * b + t + 1)
                v.reduce_max(neg_max[:, t:t + 1], scores[:, t % 2, 0:(t + 1) * P], AX.X,
                             negate=True).then_inc(max_ready, 1)

            def pt_l(b, t, h):
                dve.wait_ge(pt_high, N_PT * b + PT_NO[(t, h)] + 1)
                g, n = t // G, min(G, t + 1 - h * G)
                s = slot(g, h * G)
                q = slice((t % G) * P, (t % G + 1) * P)
                src = work_bank(b, ("PT", t, h))[:, 0:n * P].rearrange("p (k q) -> p k q", q=P)
                v.tensor_tensor(p_l[:, s:s + n, q], src, plain(p_h[:, s:s + n, q]),
                                ALU.subtract).then_inc(pt_low, 1)

            def h2_high_part(b, g):
                f = b - 1
                dve.wait_ge(h2_full, NG * f + g + 1)
                v.tensor_copy(h2_h[:, cols(g)], h2[:, cols(g)]).then_inc(h2_high, 1)

            def h1_high_part(n, g):
                dve.wait_ge(h1_full, NG * n + g + 1)
                v.tensor_copy(h1_h[:, cols(g)], h1[:, cols(g)]).then_inc(h1_high, 1)

            def invert_sums(b, g):
                dve.wait_ge(probs_ready, NT * b + G * (g + 1))
                if not at(b, 0):
                    dve.wait_ge(x1_ready, NT * (b - 1) + G * (g + 1))
                v.reciprocal(row_rec[:, G * g:G * g + G], row_sum[:, G * g:G * g + G]).then_inc(rec_ready, 1)

            def first_residual(b, g):
                count, bank = place(b, ("O", g))
                dve.wait_ge(work_ready, count)
                dve.wait_ge(rec_ready, NG * b + g + 1)
                dve.wait_ge(x_res_ready, NG * b + g + 1)
                if not at(b, 0):
                    dve.wait_ge(z2_ready, NT * (b - 1) + G * (g + 1))
                    dve.wait_ge(y_ready, NG * (b - 1) + g + 1)
                for i in range(G):
                    t = G * g + i
                    v.scalar_tensor_tensor(x1[:, t, :], work[:, bank, i * P:(i + 1) * P],
                                           row_rec[:, t:t + 1], x_res[:, t, :],
                                           ALU.mult, ALU.add).then_inc(x1_ready, 1)

            def statistics2(b, g):
                dve.wait_ge(x1_ready, NT * b + G * (g + 1))
                if not at(b, 0):
                    dve.wait_ge(z2_ready, NT * (b - 1) + G * (g + 1))
                statistics(x1, stats2, mv2, bn2, mv2_ready, b, g)

            def count_spikes(b, c, n):
                f = b - 1
                step = NUM_STEPS * (NG * f + c) + n
                if n == 0:
                    dve.wait_ge(down_done, NG * NF * f + NF * (c + 1))
                    if not at(b, 1):
                        dve.wait_ge(spikes_scaled, NG * (f - 1) + c + 1)
                    v.tensor_scalar(spikes[:, c, :], current[:, :], thetas[0], None, ALU.is_gt)\
                        .then_inc(spike_step, 1)
                else:
                    dve.wait_ge(spike_step, step)
                    v.scalar_tensor_tensor(spikes[:, c, :], current[:, :], thetas[n], spikes[:, c, :],
                                           ALU.is_gt, ALU.add).then_inc(spike_step, 1)

            def second_residual(b, c):
                f = b - 1
                count, bank = place(b, ("OT", c))
                dve.wait_ge(work_ready, count)
                if not at(b, 1):
                    dve.wait_ge(stored[c], 16 * f)
                v.tensor_tensor(y_out[:, c, :, :], work[:, bank, :].rearrange("p (t d) -> p t d", d=D),
                                x1[:, G * c:G * c + G, :], ALU.add).then_inc(y_ready, 1)

            for g in range(NG):
                statistics1(0, g)

            done = [0]

            def link(instruction):
                done[0] += 1
                instruction.then_inc(prep, 1)
                dve.wait_ge(prep, done[0])

            dve.wait_ge(silu_step, 1)
            v.tensor_scalar_add(silu_rec[:, :], silu_den[:, :], 1.0).then_inc(silu_step, 1)
            dve.wait_ge(silu_step, 2)
            v.reciprocal(silu_den[:, :], silu_rec[:, :]).then_inc(silu_step, 1)
            dve.wait_ge(silu_step, 3)
            link(v.tensor_tensor(silu[:, :], ct_sb[:, :], silu_den[:, :], ALU.mult))
            link(v.tensor_copy(bcast[:, :, :], silu[:, :].unsqueeze(2).to_broadcast([P, B, P])))
            dve.wait_ge(prep_mm, 5)
            raw = scores[:, 0, 0:5 * B].rearrange("p (n b) -> p n b", b=B)
            link(v.tensor_copy(mod[:, :, 0:B], raw))
            link(v.tensor_copy(bcast2[:, :, :], mod[:, SA, 0:B].unsqueeze(2).to_broadcast([P, B, P])))
            for j in (CA, CB):
                link(v.tensor_scalar_add(mod[:, j, 0:B], mod[:, j, 0:B], 1.0))
            share = 1.0 / NUM_STEPS
            link(v.tensor_scalar(gb_sign[:, :], mod[:, GB, 0:B], 0.0, 2.0 * share, ALU.is_ge, ALU.mult))
            link(v.tensor_scalar(gb_size[:, :], mod[:, GB, 0:B], GATE_MIN, None, ALU.max))
            link(v.scalar_tensor_tensor(gb_size[:, :], mod[:, GB, 0:B], -1.0, gb_size[:, :],
                                        ALU.mult, ALU.max))
            link(v.scalar_tensor_tensor(mod[:, GB, 0:B], gb_sign[:, :], share, gb_size[:, :],
                                        ALU.subtract, ALU.mult))
            link(v.tensor_copy(mod[:, :, B:B + 1], mod[:, :, 0:1]))
            dve.wait_ge(prep_mm, 5 + B)
            link(v.tensor_scalar(gate_sign[:, :], scores[:, 1, :], 0.0, 2.0, ALU.is_ge, ALU.mult))
            link(v.tensor_scalar(gate_size[:, :], scores[:, 1, :], GATE_MIN, None, ALU.max))
            link(v.scalar_tensor_tensor(gate_size[:, :], scores[:, 1, :], -1.0, gate_size[:, :],
                                        ALU.mult, ALU.max))
            link(v.scalar_tensor_tensor(ga_rows[:, :, :].rearrange("p b d -> p (b d)"), gate_sign[:, :], 1.0,
                                        gate_size[:, :], ALU.subtract, ALU.mult))
            dve.wait_ge(w_loaded, 8 * 16)
            for b in range(B):
                last = v.tensor_scalar(wv_scaled[:, b, :], wv_sb[:, :], mod[:, CA, b:b + 1], None, ALU.mult)
            link(last)
            link(v.tensor_tensor(wv_out[:, :, :], wv_scaled[:, :, :], ga_rows[:, :, :], ALU.mult))
            dve.wait_ge(prep_mm, 5 + 2 * B)
            link(v.tensor_tensor(bias_rows[:, :, :], scores[:, 0, :].rearrange("p (b d) -> p b d", d=D),
                                 ga_rows[:, :, :], ALU.mult))
            link(v.tensor_scalar(wq_s[:, :], wq_sb[:, :], QK_SCALE, None, ALU.mult))
            link(v.tensor_scalar(bq_s[:, :], bq_sb[:, :], QK_SCALE, None, ALU.mult))
            for full, high, low in ((wq_s, wq_h, wq_l), (wk_sb, wk_h, wk_l), (wfc_sb, wfc_h, wfc_l)):
                link(v.tensor_copy(high[:, :], full[:, :]))
                link(v.tensor_tensor(low[:, :], full[:, :], plain(high[:, :]), ALU.subtract))
            zero = slice(W - 2 * P, W - P)
            for part in (p_h, p_l):
                link(v.memset(plain(part[:, NS - 1, zero]), 0.0))
            assert done[0] == N_PREP, done[0]

            for g in range(NG):
                h1_high_part(0, g)

            def iteration(b, ffn=True, attention=True):
                if attention:
                    for g in range(NG):
                        qk_l(b, "q", g)
                        qk_l(b, "k", g)
                    maximum(b, 0)
                    maximum(b, 1)
                if ffn:
                    for g in range(NG):
                        h2_high_part(b, g)
                if attention:
                    for t in range(G):
                        pt_l(b, t, 0)
                        maximum(b, t + 2)
                    invert_sums(b, 0)
                if ffn:
                    count_spikes(b, 0, 0)
                if attention:
                    pt_l(b, 4, 0)
                    pt_l(b, 4, 1)
                    maximum(b, 6)
                    statistics1(b + 1, 0)
                if ffn:
                    count_spikes(b, 0, 1)
                    count_spikes(b, 0, 2)
                if attention:
                    pt_l(b, 5, 0)
                    pt_l(b, 5, 1)
                    maximum(b, 7)
                if ffn:
                    count_spikes(b, 0, 3)
                    count_spikes(b, 0, 4)
                if attention:
                    pt_l(b, 6, 0)
                    pt_l(b, 6, 1)
                    statistics1(b + 1, 1)
                if ffn:
                    second_residual(b, 0)
                if attention:
                    first_residual(b, 0)
                    pt_l(b, 7, 0)
                    pt_l(b, 7, 1)
                    invert_sums(b, 1)
                    for g in range(NG):
                        h1_high_part(b + 1, g)
                if ffn:
                    for n in range(NUM_STEPS):
                        count_spikes(b, 1, n)
                if attention:
                    statistics2(b, 0)
                if ffn:
                    second_residual(b, 1)
                if attention:
                    first_residual(b, 1)
                    statistics2(b, 1)

            iteration(0, ffn=False)
            iteration(1)
            with dve.Fori(2, B) as b:
                iteration(b)
            iteration(B, attention=False)

        @block.gpsimd
        def _(pool):
            g_ = nc.gpsimd
            g_.memset(ident[:, :], 0.0).then_inc(const_step, 1)
            g_.memset(mask16[:, :], 0.0).then_inc(const_step, 1)
            g_.memset(minus_half[:, :], -0.5).then_inc(const_step, 1)
            g_.memset(ones[:, :], 1.0).then_inc(const_step, 1)
            pool.wait_ge(const_step, 4)
            g_.affine_select(out=ident[:, :], in_=ident[:, :], compare_op=ALU.not_equal, fill=1.0,
                             base=0, pattern=[[-1, P]], channel_multiplier=1).then_inc(const_step, 1)
            g_.affine_select(out=mask16[:, :], in_=mask16[:, :], compare_op=ALU.is_ge, fill=MASKED,
                             base=0, pattern=[[-1, P]], channel_multiplier=1).then_inc(const_step, 1)
            pool.wait_ge(const_step, 6)
            g_.tensor_copy(ident16[:, :], ident[:, :]).then_inc(const_step, 1)

            def waited():
                pool.sem_inc(pool_waited, 1)

            def normalise(src, z, mv, var, rstd, step, counted, ready_, n, g):
                pool.wait_ge(counted, NT * n + G * (g + 1))
                own = slice(G * g, G * g + G)
                waited()
                g_.tensor_scalar_add(var[:, own], mv[:, own, 1], LN_EPS).then_inc(step, 1)
                pool.wait_ge(step, 2 * (NG * n + g) + 1)
                g_.tensor_tensor(rstd[:, own], var[:, own], minus_half[:, :], ALU.pow).then_inc(step, 1)
                pool.wait_ge(step, 2 * (NG * n + g) + 2)
                waited()
                for i in range(G * g, G * g + G):
                    g_.tensor_scalar(z[:, i, :], src[:, i, :], mv[:, i, 0:1], rstd[:, i:i + 1],
                                     ALU.subtract, ALU.mult).then_inc(ready_, 1)

            def normalise1(n, g):
                normalise(x_in, z1, mv1, var1, rstd1, rstd1_step, mv1_ready, z1_ready, n, g)

            def normalise2(b, g):
                normalise(x1, z2, mv2, var2, rstd2, rstd2_step, mv2_ready, z2_ready, b, g)

            def h1_low_part(n, g):
                pool.wait_ge(h1_high, NG * n + g + 1)
                g_.tensor_tensor(h1_l[:, cols(g)], h1[:, cols(g)], plain(h1_h[:, cols(g)]),
                                 ALU.subtract).then_inc(h1_low, 1)

            def h2_low_part(b, g):
                f = b - 1
                pool.wait_ge(h2_high, NG * f + g + 1)
                g_.tensor_tensor(h2_l[:, cols(g)], h2[:, cols(g)], plain(h2_h[:, cols(g)]),
                                 ALU.subtract).then_inc(h2_low, 1)

            def split_z1_high(b, g):
                own = slice(G * g, G * g + G)
                if not at(b, 0):
                    pool.wait_ge(acc_ready, NG * b)
                pool.wait_ge(z1_ready, NT * b + G * (g + 1))
                waited()
                g_.tensor_scalar(z1_h[:, own, :], z1[:, own, :], 1.0, None, ALU.mult).then_inc(z1_high, 1)

            def split_z1_low(b, g):
                own = slice(G * g, G * g + G)
                pool.wait_ge(z1_high, NG * b + g + 1)
                g_.tensor_tensor(z1_l[:, own, :], z1[:, own, :], plain(z1_h[:, own, :]),
                                 ALU.subtract).then_inc(z1_low, 1)

            def add_bias_row(b, g):
                pool.wait_ge(x_loaded, 16 * (b + 1))
                if not at(b, 0):
                    pool.wait_ge(x1_ready, NT * (b - 1) + G * (g + 1))
                waited()
                for i in range(G * g, G * g + G):
                    last = g_.tensor_tensor(x_res[:, i, :], x_in[:, i, :], bias_rows[:, b, :], ALU.add)
                last.then_inc(x_res_ready, 1)

            def square(b, c, j):
                n = NG * NF * (b - 1) + NF * c + j
                pool.wait_ge(relu_ready, n + 1)
                if not (at(b, 1) and c == 0 and j < 2):
                    pool.wait_ge(down_done, n - 1)
                g_.tensor_tensor(act2[:, j % 2, :], relu[:, j % 2, :], relu[:, j % 2, :],
                                 ALU.mult).then_inc(act2_ready, 1)

            for g in range(NG):
                normalise1(0, g)
            for g in range(NG):
                h1_low_part(0, g)
            pool.wait_ge(prep, N_PREP)

            def iteration(b, ffn=True, attention=True):
                if attention:
                    split_z1_high(b, 0)
                if ffn:
                    h2_low_part(b, 0)
                if attention:
                    split_z1_low(b, 0)
                if ffn:
                    square(b, 0, 0)
                if attention:
                    add_bias_row(b, 0)
                if ffn:
                    square(b, 0, 1)
                if attention:
                    add_bias_row(b, 1)
                if ffn:
                    square(b, 0, 2)
                    h2_low_part(b, 1)
                    square(b, 0, 3)
                if attention:
                    split_z1_high(b, 1)
                    split_z1_low(b, 1)
                if ffn:
                    square(b, 1, 0)
                if attention:
                    normalise1(b + 1, 0)
                if ffn:
                    square(b, 1, 1)
                if attention:
                    normalise1(b + 1, 1)
                if ffn:
                    square(b, 1, 2)
                    square(b, 1, 3)
                if attention:
                    for g in range(NG):
                        h1_low_part(b + 1, g)
                    for g in range(NG):
                        normalise2(b, g)

            iteration(0, ffn=False)
            iteration(1)
            with pool.Fori(2, B) as b:
                iteration(b)
            iteration(B, attention=False)


def kernel(**inputs):
    import concourse.bacc as _bacc
    from concourse.bass_utils import run_bass_kernel_spmd as _run

    def get(name):
        return np.asarray(inputs[name])

    w_proj = get("L0_ffn_W_proj")
    d, f = w_proj.shape
    arrays = {
        "x": get("L0_attn_x"),
        "c_t": get("L0_c").T,
        "w_mod": get("L0_wmod"),
        "wq_t": get("L0_attn_Wq").T,
        "wk_t": get("L0_attn_Wk").T,
        "wv_t": get("L0_attn_Wv").T,
        "w_fc_t": get("L0_ffn_W_fc").T,
        "w_proj_t": w_proj.T.reshape(f // 128, 128, d).transpose(1, 0, 2),
        "bq": get("L0_attn_bq").reshape(-1, 1),
        "bk": get("L0_attn_bk").reshape(-1, 1),
        "bv": get("L0_attn_bv").reshape(1, -1),
    }
    arrays = {k: np.ascontiguousarray(a) for k, a in arrays.items()}
    nc = _bacc.Bacc("TRN2", target_bir_lowering=False, num_devices=1)
    args = [nc.dram_tensor(k, a.shape, mybir.dt.from_np(a.dtype), kind="ExternalInput").ap()
            for k, a in arrays.items()]
    args.append(nc.dram_tensor("out", arrays["x"].shape, F32, kind="ExternalOutput").ap())
    build(nc, *args)
    return _run(nc, [arrays], core_ids=[0]).results[0]["out"]
```

```python
import numpy as np
import concourse.bass as bass
from concourse import mybir
from contextlib import ExitStack

F32 = mybir.dt.float32
F32R = mybir.dt.float32r
BF16 = mybir.dt.bfloat16
ALU = mybir.AluOpType
ACT = mybir.ActivationFunctionType
AX = mybir.AxisListType

BETA, THRESHOLD, NUM_STEPS = 0.9, 1.0, 5
LN_EPS = 1e-5
GATE_MIN = 0.25
MASKED = -1e38


def spike_thresholds():
    one = np.float32(1)

    def spikes(current):
        mem, count = np.float32(0), 0
        for _ in range(NUM_STEPS):
            reset = one if mem > np.float32(THRESHOLD) else np.float32(0)
            mem = np.float32(BETA) * mem + current - reset * np.float32(THRESHOLD)
            count += int(mem > np.float32(THRESHOLD))
        return count

    thetas = []
    for n in range(NUM_STEPS):
        below = int(np.float32(0).view(np.int32))
        above = int(np.float32(2).view(np.int32))
        while above - below > 1:
            mid = (below + above) // 2
            if spikes(np.int32(mid).view(np.float32)) > n:
                above = mid
            else:
                below = mid
        thetas.append(float(np.int32(below).view(np.float32)))
    return thetas


def build(nc, x, c_t, w_mod, wq_t, wk_t, wv_t, w_fc_t, w_proj_t, bq, bk, bv, out):
    B, T, D = x.shape
    P = 128
    assert D == P and T % 512 == 0
    NT = T // P
    G = 4
    NG = NT // G
    W = G * P
    F = w_fc_t.shape[1]
    NF = F // P
    SHIFTA, SCALEA, GATEA, SHIFTB, SCALEB, GATEB = range(6)
    QK_SCALE = float(D) ** -0.5
    thetas = spike_thresholds()

    x_v = x.rearrange("b (t p) d -> b p t d", p=P)
    out_v = out.rearrange("b (t p) d -> b p t d", p=P)

    RING = 4
    WORK_ORDER = [
        ("QK", "q", 0), ("QK", "k", 0), ("QK", "q", 1), ("FC", 0, 0), ("QK", "k", 1), ("FC", 0, 1),
        ("FC", 0, 2), ("PT", 0, 0), ("FC", 0, 3), ("PT", 1, 0), ("PT", 2, 0), ("PT", 3, 0), ("DN", 0),
        ("T2", 1), ("PT", 4, 0), ("A", 0), ("PT", 4, 1), ("FC", 1, 0), ("PT", 5, 0), ("PT", 5, 1),
        ("FC", 1, 1), ("FC", 1, 2), ("PT", 6, 0), ("PT", 6, 1), ("OT", 0), ("FC", 1, 3), ("O", 0),
        ("PT", 7, 0), ("PT", 7, 1), ("DN", 1), ("T1", 0), ("T1", 1), ("A", 1), ("T2", 0), ("OT", 1),
        ("O", 1),
    ]
    pt_slots = [(t, h) for t in range(NT) for h in range(t // G + 1)]
    FFN_ONLY = [s for s in WORK_ORDER if s[0] in ("FC", "DN", "OT") or s == ("T2", 1)]
    ATTENTION_ONLY = [s for s in WORK_ORDER if s not in FFN_ONLY]
    BEFORE_LOOP = [("T1", g) for g in range(NG)]
    assert len(WORK_ORDER) % RING == 0
    PT_NO = {s: n for n, s in enumerate(pt_slots)}
    N_PT = len(PT_NO)
    N_PREP = 28

    def at(b, n):
        return isinstance(b, int) and b == n

    def order_of(b):
        return ATTENTION_ONLY if at(b, 0) else FFN_ONLY if at(b, B) else WORK_ORDER

    def place(b, step):
        i = order_of(b).index(step)
        if at(b, 0):
            before = bank = len(BEFORE_LOOP)
        else:
            bank = len(BEFORE_LOOP) + len(ATTENTION_ONLY)
            before = (b - 1) * len(WORK_ORDER) + bank
        return before + i + 1, (bank + i) % RING

    ctx = ExitStack()
    with ctx:
        def sb(name, shape, dt=F32):
            return ctx.enter_context(nc.sbuf_tensor(name, shape, dt))

        def pb(name, shape):
            return ctx.enter_context(nc.psum_tensor(name, shape, F32))

        def sem(name):
            return ctx.enter_context(nc.semaphore(name))

        ident = sb("ident", [P, P])
        ident16 = sb("ident16", [P, P], BF16)
        mask16 = sb("mask16", [P, P], BF16)
        ones = sb("ones", [1, P])
        minus_half = sb("minus_half", [P, G])
        ct_sb = sb("ct_sb", [P, B])
        silu_den = sb("silu_den", [P, B])
        silu_rec = sb("silu_rec", [P, B])
        silu = sb("silu", [P, B])
        wmod_sb = sb("wmod_sb", [P, 6 * D])
        wq_sb = sb("wq_sb", [P, D])
        wk_sb = sb("wk_sb", [P, D])
        wv_sb = sb("wv_sb", [P, D])
        wfc_sb = sb("wfc_sb", [P, F])
        wproj_sb = sb("wproj_sb", [P, NF, D])
        bq_sb = sb("bq_sb", [P, 1])
        bk_sb = sb("bk_sb", [P, 1])
        bv_sb = sb("bv_sb", [1, D])
        wq_s = sb("wq_s", [P, D])
        bq_s = sb("bq_s", [P, 1])
        wq_h, wq_l = sb("wq_h", [P, D], F32R), sb("wq_l", [P, D], F32R)
        wk_h, wk_l = sb("wk_h", [P, D], F32R), sb("wk_l", [P, D], F32R)
        wfc_h, wfc_l = sb("wfc_h", [P, F], F32R), sb("wfc_l", [P, F], F32R)
        mod = sb("mod", [P, 5, B + 1])
        CA, SA, CB, SB, GB = range(5)
        gate_sign = sb("gate_sign", [P, B * D])
        gate_size = sb("gate_size", [P, B * D])
        ga_rows = sb("ga_rows", [P, B, D])
        bcast = sb("bcast", [P, B, P])
        bcast2 = sb("bcast2", [P, B, P])
        wv_scaled = sb("wv_scaled", [P, B, D])
        wv_out = sb("wv_out", [P, B, D])
        bias_rows = sb("bias_rows", [P, B, D])
        gb_sign = sb("gb_sign", [P, B])
        gb_size = sb("gb_size", [P, B])

        x_in = sb("x_in", [P, NT, D])
        x_res = sb("x_res", [P, NT, D])
        z1 = sb("z1", [P, NT, D])
        z1_h, z1_l = sb("z1_h", [P, NT, D], F32R), sb("z1_l", [P, NT, D], F32R)
        h1 = sb("h1", [P, T])
        h1_h, h1_l = sb("h1_h", [P, T], F32R), sb("h1_l", [P, T], F32R)
        q_h, q_l = sb("q_h", [P, T], F32R), sb("q_l", [P, T], F32R)
        k_h, k_l = sb("k_h", [P, T], F32R), sb("k_l", [P, T], F32R)
        probs = sb("probs", [P, 2, T])
        NS = NT
        p_h, p_l = sb("p_h", [P, NS, W], F32R), sb("p_l", [P, NS, W], F32R)
        attended = sb("attended", [P, NG, W])
        x1 = sb("x1", [P, NT, D])
        z2 = sb("z2", [P, NT, D])
        h2 = sb("h2", [P, T])
        h2_h, h2_l = sb("h2_h", [P, T], F32R), sb("h2_l", [P, T], F32R)
        relu = sb("relu", [P, NF, W])
        act2 = sb("act2", [P, NF, W])
        current = sb("current", [P, NG, W])
        spikes = sb("spikes", [P, 2, W])
        spikes_g = sb("spikes_g", [P, 2, W])
        y_out = sb("y_out", [P, NG, G, D])
        neg_max = sb("neg_max", [P, NT])
        row_sum = sb("row_sum", [P, NT])
        row_rec = sb("row_rec", [P, NT])
        stats1, stats2 = sb("stats1", [P, NT, 6]), sb("stats2", [P, NT, 6])
        mv1, mv2 = sb("mv1", [P, NT, 2]), sb("mv2", [P, NT, 2])
        var1, var2 = sb("var1", [P, NT]), sb("var2", [P, NT])
        rstd1, rstd2 = sb("rstd1", [P, NT]), sb("rstd2", [P, NT])
        shift1, shift2 = sb("shift1", [P, NT]), sb("shift2", [P, NT])

        scores = pb("scores", [P, 2, T])
        work = pb("work", [P, RING, W])

        c_loaded, w_loaded, x_loaded = sem("c_loaded"), sem("w_loaded"), sem("x_loaded")
        stored = [sem(f"stored{g}") for g in range(NG)]
        const_step = sem("const_step")
        silu_step = sem("silu_step")
        act_waited, dve_waited, pool_waited = sem("act_waited"), sem("dve_waited"), sem("pool_waited")
        prep = sem("prep")
        prep_mm = sem("prep_mm")
        work_ready = sem("work_ready")
        scores_ready = sem("scores_ready")
        qk_high, qk_low = sem("qk_high"), sem("qk_low")
        probs_ready = sem("probs_ready")
        pt_high, pt_low = sem("pt_high"), sem("pt_low")
        attended_ready = sem("attended_ready")
        h1_full, h1_high, h1_low = sem("h1_full"), sem("h1_high"), sem("h1_low")
        h2_full, h2_high, h2_low = sem("h2_full"), sem("h2_high"), sem("h2_low")
        relu_ready, act2_ready = sem("relu_ready"), sem("act2_ready")
        current_ready = sem("current_ready")
        spike_step = sem("spike_step")
        spikes_scaled = sem("spikes_scaled")
        y_ready = sem("y_ready")
        max_ready = sem("max_ready")
        rec_ready = sem("rec_ready")
        x1_ready = sem("x1_ready")
        bn1, bn2 = sem("bn1"), sem("bn2")
        mv1_ready, mv2_ready = sem("mv1_ready"), sem("mv2_ready")
        rstd1_step, rstd2_step = sem("rstd1_step"), sem("rstd2_step")
        z1_ready, z2_ready = sem("z1_ready"), sem("z2_ready")
        z1_high, z1_low = sem("z1_high"), sem("z1_low")
        x_res_ready = sem("x_res_ready")

        block = ctx.enter_context(nc.Block())

        def cols(g):
            return slice(g * W, (g + 1) * W)

        def slot(g, kt):
            return kt + (NS - G * (g + 1))

        def halves(g, half):
            first = G * g + half * (G // 2)
            return range(first, first + G // 2)

        def plain(ap):
            return ap.bitcast(F32)

        @block.sync
        def _(sp):
            sp.dma_start(ct_sb[:, :], c_t).then_inc(c_loaded, 16)
            sp.dma_start(wmod_sb[:, :], w_mod).then_inc(c_loaded, 16)
            sp.dma_start(x_in[:, :, :], x_v[0]).then_inc(x_loaded, 16)
            for dst, src in ((wq_sb, wq_t), (wk_sb, wk_t), (wv_sb, wv_t), (wfc_sb, w_fc_t),
                             (bq_sb, bq), (bk_sb, bk), (bv_sb, bv)):
                sp.dma_start(dst[:, :], src).then_inc(w_loaded, 16)
            sp.dma_start(wproj_sb[:, :, :], w_proj_t).then_inc(w_loaded, 16)

            def next_x(b, src):
                sp.wait_ge(x_res_ready, NG * b + NG)
                sp.wait_ge(z1_ready, NT * b + NT)
                sp.dma_start(x_in[:, :, :], src).then_inc(x_loaded, 16)

            def store(f, g):
                sp.wait_ge(y_ready, NG * f + g + 1)
                sp.dma_start(out_v[f][:, g * G:(g + 1) * G, :], y_out[:, g, :, :]).then_inc(stored[g], 16)

            next_x(0, x_v[1])
            with sp.Fori(1, B - 1) as b:
                next_x(b, x_v[b + 1])
                for g in range(NG):
                    store(b - 1, g)
            next_x(B - 1, x_v[0])
            for f in (B - 2, B - 1):
                for g in range(NG):
                    store(f, g)
            for g in range(NG):
                sp.wait_ge(stored[g], 16 * B)
            sp.wait_ge(x_loaded, 16 * (B + 1))

        @block.tensor
        def _(pe):
            mm = nc.tensor.matmul

            def three(dst, a_h, a_l, b_h, b_l, start=True, stop=True):
                mm(dst, a_h, b_h, start=start, stop=False)
                mm(dst, a_l, b_h, start=False, stop=False)
                return mm(dst, a_h, b_l, start=False, stop=stop)

            pe.wait_ge(const_step, 7)
            pe.wait_ge(prep, 1)
            pe.wait_ge(c_loaded, 32)
            for n, j in enumerate((SCALEA, SHIFTA, SCALEB, SHIFTB, GATEB)):
                mm(scores[:, 0, n * B:(n + 1) * B], wmod_sb[:, j * D:(j + 1) * D], silu[:, :],
                   start=True, stop=True).then_inc(prep_mm, 1)
            pe.wait_ge(prep, 2)
            for b in range(B):
                mm(scores[:, 1, b * D:(b + 1) * D], bcast[:, b, :],
                   wmod_sb[:, GATEA * D:(GATEA + 1) * D], start=True, stop=True).then_inc(prep_mm, 1)
            pe.wait_ge(prep, 4)
            pe.wait_ge(w_loaded, 8 * 16)
            for b in range(B):
                dst = scores[:, 0, b * D:(b + 1) * D]
                mm(dst, bcast2[:, b, :], wv_sb[:, :], start=True, stop=False)
                mm(dst, ones[:, :], bv_sb[:, :], start=False, stop=True).then_inc(prep_mm, 1)

            def bank_reader(b, step):
                kind, rest = step[0], step[1:]
                if kind == "QK":
                    return qk_low, 2 * NG * b + 2 * rest[1] + (rest[0] == "k") + 1
                if kind == "PT":
                    return pt_low, N_PT * b + PT_NO[rest] + 1
                if kind == "A":
                    return attended_ready, NG * b + rest[0] + 1
                if kind == "O":
                    return x1_ready, NT * b + G * (rest[0] + 1)
                if kind == "T1":
                    return h1_full, NG * (b + 1) + rest[0] + 1
                if kind == "T2":
                    return h2_full, NG * (b - rest[0]) + rest[0] + 1
                if kind == "FC":
                    return relu_ready, NG * NF * (b - 1) + NF * rest[0] + rest[1] + 1
                if kind == "DN":
                    return current_ready, NG * (b - 1) + rest[0] + 1
                return y_ready, NG * (b - 1) + rest[0] + 1

            def work_tile(b, step):
                i = order_of(b).index(step)
                if i >= RING:
                    pe.wait_ge(*bank_reader(b, order_of(b)[i - RING]))
                elif at(b, 0):
                    if i >= RING - len(BEFORE_LOOP):
                        pe.wait_ge(*bank_reader(-1, BEFORE_LOOP[i - RING]))
                else:
                    last = ATTENTION_ONLY if at(b, 1) else WORK_ORDER
                    pe.wait_ge(*bank_reader(b - 1, last[i - RING]))
                return work[:, place(b, step)[1], :]

            def rows_to_columns(dst, src, g):
                for i in range(G):
                    last = nc.tensor.transpose(dst[:, i * P:(i + 1) * P], src[:, g * G + i, :], ident[:, :])
                return last

            def t1(n, g, dst):
                pe.wait_ge(z1_ready, NT * n + G * (g + 1))
                rows_to_columns(dst, z1, g).then_inc(work_ready, 1)

            for g in range(NG):
                t1(0, g, work[:, g, :])
            pe.wait_ge(prep, N_PREP)

            def qk(b, which, g):
                w_h, w_l = (wq_h, wq_l) if which == "q" else (wk_h, wk_l)
                dst = work_tile(b, ("QK", which, g))
                pe.wait_ge(h1_high, NG * b + g + 1)
                pe.wait_ge(h1_low, NG * b + g + 1)
                three(dst, w_h[:, :], w_l[:, :], h1_h[:, cols(g)], h1_l[:, cols(g)]).then_inc(work_ready, 1)

            def score(b, t):
                g = t // G
                pe.wait_ge(qk_low, 2 * NG * b + 2 * g + 2)
                if not (at(b, 0) and t < 2):
                    pe.wait_ge(probs_ready, NT * b + t - 1)
                width = (t + 1) * P
                rows = slice(t * P, (t + 1) * P)
                for lo in range(0, width, W):
                    n = max(min(width - lo, W), 2 * P)
                    diagonal = lo + W >= width
                    three(scores[:, t % 2, lo:lo + n], q_h[:, rows], q_l[:, rows],
                          k_h[:, lo:lo + n], k_l[:, lo:lo + n], stop=not diagonal)
                last = mm(scores[:, t % 2, t * P:width], ident16[:, :], mask16[:, :],
                          start=False, stop=True)
                last.then_inc(scores_ready, 1)

            def transpose_probs(b, t, h):
                dst = work_tile(b, ("PT", t, h))
                pe.wait_ge(probs_ready, NT * b + t + 1)
                blocks = range(h * G, min(h * G + G, t + 1))
                for kt in blocks:
                    last = nc.tensor.transpose(dst[:, (kt - h * G) * P:(kt - h * G + 1) * P],
                                               probs[:, t % 2, kt * P:(kt + 1) * P], ident[:, :])
                last.then_inc(work_ready, 1)

            def attend(b, g):
                dst = work_tile(b, ("A", g))
                pe.wait_ge(pt_low, N_PT * b + PT_NO[(G * g + G - 1, g)] + 1)
                pe.wait_ge(z1_low, NG * b + g + 1)
                last_kt = G * (g + 1) - 1
                for kt in range(last_kt + 1):
                    c0 = min(max(kt - G * g, 0) * P, W - 2 * P)
                    s = slot(g, kt)
                    last = three(dst[:, c0:W], z1_h[:, kt, :], z1_l[:, kt, :],
                                 p_h[:, s, c0:W], p_l[:, s, c0:W], start=kt == 0, stop=kt == last_kt)
                last.then_inc(work_ready, 1)

            def project_out(b, g):
                dst = work_tile(b, ("O", g))
                pe.wait_ge(attended_ready, NG * b + g + 1)
                for i in range(G):
                    last = mm(dst[:, i * P:(i + 1) * P], attended[:, g, i * P:(i + 1) * P],
                              wv_out[:, b, :], start=True, stop=True)
                last.then_inc(work_ready, 1)

            def t2(b, g):
                dst = work_tile(b, ("T2", g))
                pe.wait_ge(z2_ready, NT * (b - g) + G * (g + 1))
                rows_to_columns(dst, z2, g).then_inc(work_ready, 1)

            def up(b, c, j):
                dst = work_tile(b, ("FC", c, j))
                pe.wait_ge(h2_high, NG * (b - 1) + c + 1)
                pe.wait_ge(h2_low, NG * (b - 1) + c + 1)
                w = slice(j * P, (j + 1) * P)
                three(dst, wfc_h[:, w], wfc_l[:, w], h2_h[:, cols(c)], h2_l[:, cols(c)])\
                    .then_inc(work_ready, 1)

            def down(b, c):
                dst = work_tile(b, ("DN", c))
                for j in range(NF):
                    pe.wait_ge(act2_ready, NG * NF * (b - 1) + NF * c + j + 1)
                    last = mm(dst, wproj_sb[:, j, :], act2[:, j, :], start=j == 0, stop=j == NF - 1)
                last.then_inc(work_ready, 1)

            def spikes_back(b, c):
                dst = work_tile(b, ("OT", c))
                pe.wait_ge(spikes_scaled, NG * (b - 1) + c + 1)
                for i in range(G):
                    last = nc.tensor.transpose(dst[:, i * P:(i + 1) * P],
                                               spikes_g[:, c, i * P:(i + 1) * P], ident[:, :])
                last.then_inc(work_ready, 1)

            def iteration(b, ffn=True, attention=True):
                if attention:
                    qk(b, "q", 0)
                    qk(b, "k", 0)
                    qk(b, "q", 1)
                if ffn:
                    up(b, 0, 0)
                if attention:
                    qk(b, "k", 1)
                    score(b, 0)
                    score(b, 1)
                if ffn:
                    up(b, 0, 1)
                    up(b, 0, 2)
                if attention:
                    score(b, 2)
                    transpose_probs(b, 0, 0)
                    score(b, 3)
                if ffn:
                    up(b, 0, 3)
                if attention:
                    transpose_probs(b, 1, 0)
                    score(b, 4)
                    transpose_probs(b, 2, 0)
                    score(b, 5)
                    transpose_probs(b, 3, 0)
                if ffn:
                    down(b, 0)
                    t2(b, 1)
                if attention:
                    score(b, 6)
                    transpose_probs(b, 4, 0)
                    attend(b, 0)
                    transpose_probs(b, 4, 1)
                if ffn:
                    up(b, 1, 0)
                if attention:
                    transpose_probs(b, 5, 0)
                    transpose_probs(b, 5, 1)
                if ffn:
                    up(b, 1, 1)
                if attention:
                    score(b, 7)
                if ffn:
                    up(b, 1, 2)
                if attention:
                    transpose_probs(b, 6, 0)
                    transpose_probs(b, 6, 1)
                if ffn:
                    spikes_back(b, 0)
                    up(b, 1, 3)
                if attention:
                    project_out(b, 0)
                    transpose_probs(b, 7, 0)
                    transpose_probs(b, 7, 1)
                if ffn:
                    down(b, 1)
                if attention:
                    t1(b + 1, 0, work_tile(b, ("T1", 0)))
                    t1(b + 1, 1, work_tile(b, ("T1", 1)))
                    attend(b, 1)
                    t2(b, 0)
                if ffn:
                    spikes_back(b, 1)
                if attention:
                    project_out(b, 1)

            iteration(0, ffn=False)
            iteration(1)
            with pe.Fori(2, B) as b:
                iteration(b)
            iteration(B, attention=False)

        @block.scalar
        def _(act):
            act.wait_ge(c_loaded, 32)
            nc.scalar.activation(silu_den[:, :], ct_sb[:, :], ACT.Exp, scale=-1.0).then_inc(silu_step, 1)

            def ready(b, step):
                count, bank = place(b, step)
                act.wait_ge(work_ready, count)
                return work[:, bank, :]

            def waited():
                act.sem_inc(act_waited, 1)

            def qk_h(b, which, g):
                src = ready(b, ("QK", which, g))
                if g == 0 and which == "q" and not at(b, 0):
                    act.wait_ge(scores_ready, NT * b)
                dst, bias = (q_h, bq_s) if which == "q" else (k_h, bk_sb)
                nc.scalar.activation(dst[:, cols(g)], src, ACT.Identity, bias=bias[:, 0:1]).then_inc(qk_high, 1)

            def exponential(b, t):
                n = NT * b + t
                act.wait_ge(max_ready, n + 1)
                if t >= 2:
                    act.wait_ge(work_ready, place(b, ("PT", t - 2, (t - 2) // G))[0])
                elif not at(b, 0):
                    act.wait_ge(rec_ready, NG * b)
                width = (t + 1) * P
                nc.scalar.activation(probs[:, t % 2, 0:width], scores[:, t % 2, 0:width], ACT.Exp,
                                     bias=neg_max[:, t:t + 1],
                                     accum_out=row_sum[:, t:t + 1]).then_inc(probs_ready, 1)

            def pt_h(b, t, h):
                src = ready(b, ("PT", t, h))
                g, n = t // G, min(G, t + 1 - h * G)
                if (t, h) == (G, 1):
                    act.wait_ge(work_ready, place(b, ("A", 0))[0])
                elif t == 0 and not at(b, 0):
                    act.wait_ge(work_ready, place(0 if at(b, 1) else b - 1, ("A", 1))[0])
                s = slot(g, h * G)
                nc.scalar.activation(p_h[:, s:s + n, (t % G) * P:(t % G + 1) * P],
                                     src[:, 0:n * P].rearrange("p (k q) -> p k q", q=P),
                                     ACT.Copy).then_inc(pt_high, 1)

            def copy_attended(b, g):
                nc.scalar.activation(attended[:, g, :], ready(b, ("A", g)),
                                     ACT.Copy).then_inc(attended_ready, 1)

            def copy_current(b, c):
                src = ready(b, ("DN", c))
                if not at(b, 1):
                    act.wait_ge(spike_step, NUM_STEPS * (NG * (b - 2) + c + 1))
                nc.scalar.activation(current[:, c, :], src, ACT.Copy).then_inc(current_ready, 1)

            def modulate1(n, src, g):
                if not at(n, 0):
                    act.wait_ge(h1_low, NG * (n - 1) + g + 1)
                waited()
                nc.scalar.activation(h1[:, cols(g)], src, ACT.Identity, bias=mod[:, SA, bass.ds(n, 1)],
                                     scale=mod[:, CA, bass.ds(n, 1)]).then_inc(h1_full, 1)

            def modulate2(b, g):
                src = ready(b, ("T2", g))
                n = b - g
                if not at(n, 0):
                    act.wait_ge(h2_low, NG * (n - 1) + g + 1)
                waited()
                nc.scalar.activation(h2[:, cols(g)], src, ACT.Identity, bias=mod[:, SB, bass.ds(n, 1)],
                                     scale=mod[:, CB, bass.ds(n, 1)]).then_inc(h2_full, 1)

            def rectify(b, c, j):
                src = ready(b, ("FC", c, j))
                if not (at(b, 1) and c == 0):
                    act.wait_ge(act2_ready, NF * (NG * (b - 1) + c - 1) + j + 1)
                nc.scalar.activation(relu[:, j, :], src, ACT.Relu).then_inc(relu_ready, 1)

            def scale_spikes(b, c):
                f = b - 1
                act.wait_ge(spike_step, NUM_STEPS * (NG * f + c + 1))
                waited()
                nc.scalar.activation(spikes_g[:, c, :], spikes[:, c, :], ACT.Identity,
                                     scale=mod[:, GB, bass.ds(f, 1)]).then_inc(spikes_scaled, 1)

            def normalise(src, z, rstd, shift, step, ready_, n, g, half):
                if half == 0:
                    act.wait_ge(step, 4 * (NG * n + g) + 4)
                for i in halves(g, half):
                    nc.scalar.activation(z[:, i, :], src[:, i, :], ACT.Identity, bias=shift[:, i:i + 1],
                                         scale=rstd[:, i:i + 1]).then_inc(ready_, 1)

            def normalise1(n, g, half):
                if half == 0 and not at(n, 0):
                    act.wait_ge(z1_low, NG * (n - 1) + g + 1)
                normalise(x_in, z1, rstd1, shift1, rstd1_step, z1_ready, n, g, half)

            def normalise2(n, g, half):
                normalise(x1, z2, rstd2, shift2, rstd2_step, z2_ready, n, g, half)

            for g in range(NG):
                for half in range(2):
                    normalise1(0, g, half)
            act.wait_ge(prep, N_PREP)
            for g in range(NG):
                act.wait_ge(work_ready, g + 1)
                modulate1(0, work[:, g, :], g)

            def iteration(b, ffn=True, attention=True):
                if attention:
                    qk_h(b, "q", 0)
                    qk_h(b, "k", 0)
                    qk_h(b, "q", 1)
                if ffn:
                    rectify(b, 0, 0)
                if attention:
                    qk_h(b, "k", 1)
                    exponential(b, 0)
                    exponential(b, 1)
                if ffn:
                    rectify(b, 0, 1)
                    rectify(b, 0, 2)
                if attention:
                    exponential(b, 2)
                    pt_h(b, 0, 0)
                    exponential(b, 3)
                    pt_h(b, 1, 0)
                if ffn:
                    rectify(b, 0, 3)
                if attention:
                    pt_h(b, 2, 0)
                if ffn:
                    normalise2(b - 1, 1, 0)
                    normalise2(b - 1, 1, 1)
                if attention:
                    exponential(b, 4)
                    pt_h(b, 3, 0)
                if ffn:
                    copy_current(b, 0)
                    modulate2(b, 1)
                if attention:
                    exponential(b, 5)
                    pt_h(b, 4, 0)
                    normalise1(b + 1, 0, 0)
                    copy_attended(b, 0)
                    pt_h(b, 4, 1)
                    exponential(b, 6)
                    pt_h(b, 5, 0)
                    pt_h(b, 5, 1)
                if ffn:
                    rectify(b, 1, 0)
                    rectify(b, 1, 1)
                    scale_spikes(b, 0)
                    rectify(b, 1, 2)
                if attention:
                    pt_h(b, 6, 0)
                    pt_h(b, 6, 1)
                    exponential(b, 7)
                if ffn:
                    rectify(b, 1, 3)
                if attention:
                    normalise1(b + 1, 0, 1)
                    normalise1(b + 1, 1, 0)
                    pt_h(b, 7, 0)
                    normalise1(b + 1, 1, 1)
                    pt_h(b, 7, 1)
                if ffn:
                    copy_current(b, 1)
                if attention:
                    modulate1(b + 1, ready(b, ("T1", 0)), 0)
                    normalise2(b, 0, 0)
                    modulate1(b + 1, ready(b, ("T1", 1)), 1)
                    normalise2(b, 0, 1)
                if ffn:
                    scale_spikes(b, 1)
                if attention:
                    copy_attended(b, 1)
                    modulate2(b, 0)

            iteration(0, ffn=False)
            iteration(1)
            with act.Fori(2, B) as b:
                iteration(b)
            iteration(B, attention=False)

        @block.vector
        def _(dve):
            v = nc.vector
            def waited():
                dve.sem_inc(dve_waited, 1)

            def statistics(src, stats, counted, g, half):
                for i in halves(g, half):
                    v.bn_stats(stats[:, i, :], src[:, i, :]).then_inc(counted, 1)

            def aggregate(stats, mv, counted, ready_, n, g):
                dve.wait_ge(counted, NT * n + G * (g + 1))
                waited()
                for i in range(G * g, G * g + G):
                    v.bn_aggr(mv[:, i, :], stats[:, i, :]).then_inc(ready_, 1)

            def statistics1(n, g, half):
                if g == 0 and half == 0:
                    dve.wait_ge(x_loaded, 16 * (n + 1))
                    if not at(n, 0):
                        dve.wait_ge(z1_ready, NT * n)
                statistics(x_in, stats1, bn1, g, half)

            def aggregate1(n, g):
                aggregate(stats1, mv1, bn1, mv1_ready, n, g)

            def statistics2(n, g, half):
                if half == 0:
                    dve.wait_ge(x1_ready, NT * n + G * (g + 1))
                    if not at(n, 0):
                        dve.wait_ge(z2_ready, NT * (n - 1) + G * (g + 1))
                statistics(x1, stats2, bn2, g, half)

            def aggregate2(n, g):
                aggregate(stats2, mv2, bn2, mv2_ready, n, g)

            def work_bank(b, step):
                return work[:, place(b, step)[1], :]

            def qk_l(b, which, g):
                n = 2 * NG * b + 2 * g + (which == "k")
                dve.wait_ge(qk_high, n + 1)
                high, low, bias = (q_h, q_l, bq_s) if which == "q" else (k_h, k_l, bk_sb)
                v.scalar_tensor_tensor(low[:, cols(g)], work_bank(b, ("QK", which, g)), bias[:, 0:1],
                                       plain(high[:, cols(g)]), ALU.add, ALU.subtract).then_inc(qk_low, 1)

            def maximum(b, t):
                dve.wait_ge(scores_ready, NT * b + t + 1)
                v.reduce_max(neg_max[:, t:t + 1], scores[:, t % 2, 0:(t + 1) * P], AX.X,
                             negate=True).then_inc(max_ready, 1)

            def pt_l(b, t, h):
                dve.wait_ge(pt_high, N_PT * b + PT_NO[(t, h)] + 1)
                g, n = t // G, min(G, t + 1 - h * G)
                s = slot(g, h * G)
                q = slice((t % G) * P, (t % G + 1) * P)
                src = work_bank(b, ("PT", t, h))[:, 0:n * P].rearrange("p (k q) -> p k q", q=P)
                v.tensor_tensor(p_l[:, s:s + n, q], src, plain(p_h[:, s:s + n, q]),
                                ALU.subtract).then_inc(pt_low, 1)

            def h2_high_part(n, g):
                dve.wait_ge(h2_full, NG * n + g + 1)
                v.tensor_copy(h2_h[:, cols(g)], h2[:, cols(g)]).then_inc(h2_high, 1)

            def h1_high_part(n, g):
                dve.wait_ge(h1_full, NG * n + g + 1)
                v.tensor_copy(h1_h[:, cols(g)], h1[:, cols(g)]).then_inc(h1_high, 1)

            def split_z1_high(b, g):
                own = slice(G * g, G * g + G)
                if not at(b, 0):
                    dve.wait_ge(work_ready, place(0 if at(b, 1) else b - 1, ("A", NG - 1))[0])
                dve.wait_ge(z1_ready, NT * b + G * (g + 1))
                v.tensor_copy(z1_h[:, own, :], z1[:, own, :]).then_inc(z1_high, 1)

            def invert_sums(b, g):
                dve.wait_ge(probs_ready, NT * b + G * (g + 1))
                if not at(b, 0):
                    dve.wait_ge(x1_ready, NT * (b - 1) + G * (g + 1))
                v.reciprocal(row_rec[:, G * g:G * g + G], row_sum[:, G * g:G * g + G]).then_inc(rec_ready, 1)

            def first_residual(b, g, half):
                count, bank = place(b, ("O", g))
                if half == 0:
                    dve.wait_ge(work_ready, count)
                    dve.wait_ge(rec_ready, NG * b + g + 1)
                    dve.wait_ge(x_res_ready, NG * b + g + 1)
                    if not at(b, 0):
                        dve.wait_ge(z2_ready, NT * (b - 1) + G * (g + 1))
                        dve.wait_ge(y_ready, NG * (b - 1) + g + 1)
                for t in halves(g, half):
                    i = t - G * g
                    v.scalar_tensor_tensor(x1[:, t, :], work[:, bank, i * P:(i + 1) * P],
                                           row_rec[:, t:t + 1], x_res[:, t, :],
                                           ALU.mult, ALU.add).then_inc(x1_ready, 1)

            def count_spikes(b, c, n):
                f = b - 1
                step = NUM_STEPS * (NG * f + c) + n
                if n == 0:
                    dve.wait_ge(current_ready, NG * f + c + 1)
                    if not at(b, 1):
                        dve.wait_ge(spikes_scaled, NG * (f - 1) + c + 1)
                    v.tensor_scalar(spikes[:, c, :], current[:, c, :], thetas[0], None, ALU.is_gt)\
                        .then_inc(spike_step, 1)
                else:
                    dve.wait_ge(spike_step, step)
                    v.scalar_tensor_tensor(spikes[:, c, :], current[:, c, :], thetas[n], spikes[:, c, :],
                                           ALU.is_gt, ALU.add).then_inc(spike_step, 1)

            def second_residual(b, c):
                f = b - 1
                count, bank = place(b, ("OT", c))
                dve.wait_ge(work_ready, count)
                if not at(b, 1):
                    dve.wait_ge(stored[c], 16 * f)
                v.tensor_tensor(y_out[:, c, :, :], work[:, bank, :].rearrange("p (t d) -> p t d", d=D),
                                x1[:, G * c:G * c + G, :], ALU.add).then_inc(y_ready, 1)

            for g in range(NG):
                for half in range(2):
                    statistics1(0, g, half)
                aggregate1(0, g)

            done = [0]

            def link(instruction):
                done[0] += 1
                instruction.then_inc(prep, 1)
                dve.wait_ge(prep, done[0])

            dve.wait_ge(silu_step, 1)
            v.tensor_scalar_add(silu_rec[:, :], silu_den[:, :], 1.0).then_inc(silu_step, 1)
            dve.wait_ge(silu_step, 2)
            v.reciprocal(silu_den[:, :], silu_rec[:, :]).then_inc(silu_step, 1)
            dve.wait_ge(silu_step, 3)
            link(v.tensor_tensor(silu[:, :], ct_sb[:, :], silu_den[:, :], ALU.mult))
            link(v.tensor_copy(bcast[:, :, :], silu[:, :].unsqueeze(2).to_broadcast([P, B, P])))
            dve.wait_ge(prep_mm, 5)
            raw = scores[:, 0, 0:5 * B].rearrange("p (n b) -> p n b", b=B)
            link(v.tensor_copy(mod[:, :, 0:B], raw))
            link(v.tensor_copy(bcast2[:, :, :], mod[:, SA, 0:B].unsqueeze(2).to_broadcast([P, B, P])))
            for j in (CA, CB):
                link(v.tensor_scalar_add(mod[:, j, 0:B], mod[:, j, 0:B], 1.0))
            share = 1.0 / NUM_STEPS
            link(v.tensor_scalar(gb_sign[:, :], mod[:, GB, 0:B], 0.0, 2.0 * share, ALU.is_ge, ALU.mult))
            link(v.tensor_scalar(gb_size[:, :], mod[:, GB, 0:B], GATE_MIN, None, ALU.max))
            link(v.scalar_tensor_tensor(gb_size[:, :], mod[:, GB, 0:B], -1.0, gb_size[:, :],
                                        ALU.mult, ALU.max))
            link(v.scalar_tensor_tensor(mod[:, GB, 0:B], gb_sign[:, :], share, gb_size[:, :],
                                        ALU.subtract, ALU.mult))
            link(v.tensor_copy(mod[:, :, B:B + 1], mod[:, :, 0:1]))
            dve.wait_ge(prep_mm, 5 + B)
            link(v.tensor_scalar(gate_sign[:, :], scores[:, 1, :], 0.0, 2.0, ALU.is_ge, ALU.mult))
            link(v.tensor_scalar(gate_size[:, :], scores[:, 1, :], GATE_MIN, None, ALU.max))
            link(v.scalar_tensor_tensor(gate_size[:, :], scores[:, 1, :], -1.0, gate_size[:, :],
                                        ALU.mult, ALU.max))
            link(v.scalar_tensor_tensor(ga_rows[:, :, :].rearrange("p b d -> p (b d)"), gate_sign[:, :], 1.0,
                                        gate_size[:, :], ALU.subtract, ALU.mult))
            dve.wait_ge(w_loaded, 8 * 16)
            for b in range(B):
                last = v.tensor_scalar(wv_scaled[:, b, :], wv_sb[:, :], mod[:, CA, b:b + 1], None, ALU.mult)
            link(last)
            link(v.tensor_tensor(wv_out[:, :, :], wv_scaled[:, :, :], ga_rows[:, :, :], ALU.mult))
            dve.wait_ge(prep_mm, 5 + 2 * B)
            link(v.tensor_tensor(bias_rows[:, :, :], scores[:, 0, :].rearrange("p (b d) -> p b d", d=D),
                                 ga_rows[:, :, :], ALU.mult))
            link(v.tensor_scalar(wq_s[:, :], wq_sb[:, :], QK_SCALE, None, ALU.mult))
            link(v.tensor_scalar(bq_s[:, :], bq_sb[:, :], QK_SCALE, None, ALU.mult))
            for full, high, low in ((wq_s, wq_h, wq_l), (wk_sb, wk_h, wk_l), (wfc_sb, wfc_h, wfc_l)):
                link(v.tensor_copy(high[:, :], full[:, :]))
                link(v.tensor_tensor(low[:, :], full[:, :], plain(high[:, :]), ALU.subtract))
            zero = slice(W - 2 * P, W - P)
            for part in (p_h, p_l):
                link(v.memset(plain(part[:, NS - 1, zero]), 0.0))
            assert done[0] == N_PREP, done[0]

            for g in range(NG):
                h1_high_part(0, g)

            def iteration(b, ffn=True, attention=True):
                if attention:
                    qk_l(b, "q", 0)
                    qk_l(b, "k", 0)
                if ffn:
                    statistics2(b - 1, 1, 0)
                if attention:
                    qk_l(b, "q", 1)
                    maximum(b, 0)
                    maximum(b, 1)
                    qk_l(b, "k", 1)
                    maximum(b, 2)
                if ffn:
                    statistics2(b - 1, 1, 1)
                if attention:
                    maximum(b, 3)
                if ffn:
                    aggregate2(b - 1, 1)
                if attention:
                    maximum(b, 4)
                    invert_sums(b, 0)
                    pt_l(b, 0, 0)
                    pt_l(b, 1, 0)
                    maximum(b, 5)
                    split_z1_high(b, 0)
                    pt_l(b, 2, 0)
                    statistics1(b + 1, 0, 0)
                    statistics1(b + 1, 0, 1)
                    statistics1(b + 1, 1, 0)
                    aggregate1(b + 1, 0)
                    split_z1_high(b, 1)
                    pt_l(b, 3, 0)
                    statistics1(b + 1, 1, 1)
                if ffn:
                    count_spikes(b, 0, 0)
                    h2_high_part(b - 1, 1)
                if attention:
                    maximum(b, 6)
                if ffn:
                    count_spikes(b, 0, 1)
                if attention:
                    pt_l(b, 4, 0)
                if ffn:
                    count_spikes(b, 0, 2)
                if attention:
                    pt_l(b, 4, 1)
                if ffn:
                    count_spikes(b, 0, 3)
                    count_spikes(b, 0, 4)
                if attention:
                    pt_l(b, 5, 0)
                    pt_l(b, 5, 1)
                    aggregate1(b + 1, 1)
                    maximum(b, 7)
                    pt_l(b, 6, 0)
                    pt_l(b, 6, 1)
                if ffn:
                    second_residual(b, 0)
                if attention:
                    first_residual(b, 0, 0)
                    first_residual(b, 0, 1)
                    invert_sums(b, 1)
                    pt_l(b, 7, 0)
                    statistics2(b, 0, 0)
                    statistics2(b, 0, 1)
                    pt_l(b, 7, 1)
                    aggregate2(b, 0)
                if ffn:
                    count_spikes(b, 1, 0)
                    count_spikes(b, 1, 1)
                    count_spikes(b, 1, 2)
                if attention:
                    h1_high_part(b + 1, 0)
                if ffn:
                    count_spikes(b, 1, 3)
                    count_spikes(b, 1, 4)
                if attention:
                    h1_high_part(b + 1, 1)
                if ffn:
                    second_residual(b, 1)
                if attention:
                    h2_high_part(b, 0)
                    first_residual(b, 1, 0)
                    first_residual(b, 1, 1)

            iteration(0, ffn=False)
            iteration(1)
            with dve.Fori(2, B) as b:
                iteration(b)
            iteration(B, attention=False)

        @block.gpsimd
        def _(pool):
            g_ = nc.gpsimd
            g_.memset(ident[:, :], 0.0).then_inc(const_step, 1)
            g_.memset(mask16[:, :], 0.0).then_inc(const_step, 1)
            g_.memset(minus_half[:, :], -0.5).then_inc(const_step, 1)
            g_.memset(ones[:, :], 1.0).then_inc(const_step, 1)
            pool.wait_ge(const_step, 4)
            g_.affine_select(out=ident[:, :], in_=ident[:, :], compare_op=ALU.not_equal, fill=1.0,
                             base=0, pattern=[[-1, P]], channel_multiplier=1).then_inc(const_step, 1)
            g_.affine_select(out=mask16[:, :], in_=mask16[:, :], compare_op=ALU.is_ge, fill=MASKED,
                             base=0, pattern=[[-1, P]], channel_multiplier=1).then_inc(const_step, 1)
            pool.wait_ge(const_step, 6)
            g_.tensor_copy(ident16[:, :], ident[:, :]).then_inc(const_step, 1)

            def waited():
                pool.sem_inc(pool_waited, 1)

            def inverse_deviation(mv, var, rstd, shift, step, counted, n, g):
                pool.wait_ge(counted, NT * n + G * (g + 1))
                own = slice(G * g, G * g + G)
                waited()
                g_.tensor_scalar_add(var[:, own], mv[:, own, 1], LN_EPS).then_inc(step, 1)
                g_.tensor_scalar(shift[:, own], mv[:, own, 0], -1.0, None, ALU.mult).then_inc(step, 1)
                pool.wait_ge(step, 4 * (NG * n + g) + 2)
                g_.tensor_tensor(rstd[:, own], var[:, own], minus_half[:, :], ALU.pow).then_inc(step, 1)
                pool.wait_ge(step, 4 * (NG * n + g) + 3)
                g_.tensor_tensor(shift[:, own], shift[:, own], rstd[:, own], ALU.mult).then_inc(step, 1)

            def deviation1(n, g):
                inverse_deviation(mv1, var1, rstd1, shift1, rstd1_step, mv1_ready, n, g)

            def deviation2(n, g):
                inverse_deviation(mv2, var2, rstd2, shift2, rstd2_step, mv2_ready, n, g)

            def h1_low_part(n, g):
                pool.wait_ge(h1_high, NG * n + g + 1)
                g_.tensor_tensor(h1_l[:, cols(g)], h1[:, cols(g)], plain(h1_h[:, cols(g)]),
                                 ALU.subtract).then_inc(h1_low, 1)

            def h2_low_part(n, g):
                pool.wait_ge(h2_high, NG * n + g + 1)
                g_.tensor_tensor(h2_l[:, cols(g)], h2[:, cols(g)], plain(h2_h[:, cols(g)]),
                                 ALU.subtract).then_inc(h2_low, 1)

            def split_z1_low(b, g):
                own = slice(G * g, G * g + G)
                pool.wait_ge(z1_high, NG * b + g + 1)
                g_.tensor_tensor(z1_l[:, own, :], z1[:, own, :], plain(z1_h[:, own, :]),
                                 ALU.subtract).then_inc(z1_low, 1)

            def add_bias_row(b, g):
                pool.wait_ge(x_loaded, 16 * (b + 1))
                if not at(b, 0):
                    pool.wait_ge(x1_ready, NT * (b - 1) + G * (g + 1))
                waited()
                own = slice(G * g, G * g + G)
                row = bias_rows[:, b, :].unsqueeze(1).to_broadcast([P, G, D])
                g_.tensor_tensor(x_res[:, own, :], x_in[:, own, :], row, ALU.add).then_inc(x_res_ready, 1)

            def square(b, c, j):
                n = NG * NF * (b - 1) + NF * c + j
                pool.wait_ge(relu_ready, n + 1)
                if c > 0:
                    pool.wait_ge(work_ready, place(b, ("DN", c - 1))[0])
                elif not at(b, 1):
                    pool.wait_ge(work_ready, place(b - 1, ("DN", NG - 1))[0])
                g_.tensor_tensor(act2[:, j, :], relu[:, j, :], relu[:, j, :],
                                 ALU.mult).then_inc(act2_ready, 1)

            for g in range(NG):
                deviation1(0, g)
            for g in range(NG):
                h1_low_part(0, g)
            pool.wait_ge(prep, N_PREP)

            def iteration(b, ffn=True, attention=True):
                if attention:
                    add_bias_row(b, 0)
                    add_bias_row(b, 1)
                if ffn:
                    square(b, 0, 0)
                    square(b, 0, 1)
                    square(b, 0, 2)
                    deviation2(b - 1, 1)
                    square(b, 0, 3)
                if attention:
                    split_z1_low(b, 0)
                    deviation1(b + 1, 0)
                if ffn:
                    h2_low_part(b - 1, 1)
                if attention:
                    split_z1_low(b, 1)
                if ffn:
                    square(b, 1, 0)
                if attention:
                    deviation1(b + 1, 1)
                if ffn:
                    square(b, 1, 1)
                    square(b, 1, 2)
                    square(b, 1, 3)
                if attention:
                    deviation2(b, 0)
                    h1_low_part(b + 1, 0)
                    h1_low_part(b + 1, 1)
                    h2_low_part(b, 0)

            iteration(0, ffn=False)
            iteration(1)
            with pool.Fori(2, B) as b:
                iteration(b)
            iteration(B, attention=False)


def kernel(**inputs):
    import concourse.bacc as _bacc
    from concourse.bass_utils import run_bass_kernel_spmd as _run

    def get(name):
        return np.asarray(inputs[name])

    w_proj = get("L0_ffn_W_proj")
    d, f = w_proj.shape
    arrays = {
        "x": get("L0_attn_x"),
        "c_t": get("L0_c").T,
        "w_mod": get("L0_wmod"),
        "wq_t": get("L0_attn_Wq").T,
        "wk_t": get("L0_attn_Wk").T,
        "wv_t": get("L0_attn_Wv").T,
        "w_fc_t": get("L0_ffn_W_fc").T,
        "w_proj_t": w_proj.T.reshape(f // 128, 128, d).transpose(1, 0, 2),
        "bq": get("L0_attn_bq").reshape(-1, 1),
        "bk": get("L0_attn_bk").reshape(-1, 1),
        "bv": get("L0_attn_bv").reshape(1, -1),
    }
    arrays = {k: np.ascontiguousarray(a) for k, a in arrays.items()}
    nc = _bacc.Bacc("TRN2", target_bir_lowering=False, num_devices=1)
    args = [nc.dram_tensor(k, a.shape, mybir.dt.from_np(a.dtype), kind="ExternalInput").ap()
            for k, a in arrays.items()]
    args.append(nc.dram_tensor("out", arrays["x"].shape, F32, kind="ExternalOutput").ap())
    build(nc, *args)
    return _run(nc, [arrays], core_ids=[0]).results[0]["out"]
```

```python
import numpy as np
import concourse.bass as bass
from concourse import mybir
from contextlib import ExitStack

F32 = mybir.dt.float32
F32R = mybir.dt.float32r
BF16 = mybir.dt.bfloat16
ALU = mybir.AluOpType
ACT = mybir.ActivationFunctionType
AX = mybir.AxisListType

BETA, THRESHOLD, NUM_STEPS = 0.9, 1.0, 5
LN_EPS = 1e-5
GATE_MIN = 0.25
MASKED = -1e38
WARM_UP = 14


def spike_thresholds():
    one = np.float32(1)

    def spikes(current):
        mem, count = np.float32(0), 0
        for _ in range(NUM_STEPS):
            reset = one if mem > np.float32(THRESHOLD) else np.float32(0)
            mem = np.float32(BETA) * mem + current - reset * np.float32(THRESHOLD)
            count += int(mem > np.float32(THRESHOLD))
        return count

    thetas = []
    for n in range(NUM_STEPS):
        below = int(np.float32(0).view(np.int32))
        above = int(np.float32(2).view(np.int32))
        while above - below > 1:
            mid = (below + above) // 2
            if spikes(np.int32(mid).view(np.float32)) > n:
                above = mid
            else:
                below = mid
        thetas.append(float(np.int32(below).view(np.float32)))
    return thetas


def build(nc, x, c_t, w_mod, wq_t, wk_t, wv_t, w_fc_t, w_proj_t, bq, bk, bv, out):
    B, T, D = x.shape
    P = 128
    assert D == P and T % 512 == 0 and B * D == T
    NT = T // P
    G = 4
    NG = NT // G
    W = G * P
    F = w_fc_t.shape[1]
    NF = F // P
    SHIFTA, SCALEA, GATEA, SHIFTB, SCALEB, GATEB = range(6)
    QK_SCALE = float(D) ** -0.5
    thetas = spike_thresholds()

    x_v = x.rearrange("b (t p) d -> b p t d", p=P)
    out_v = out.rearrange("b (t p) d -> b p t d", p=P)

    RING = 4
    WORK_ORDER = [
        ("QK", "q", 0), ("QK", "k", 0), ("QK", "q", 1), ("FC", 0, 0), ("QK", "k", 1), ("FC", 0, 1),
        ("FC", 0, 2), ("PT", 0, 0), ("FC", 0, 3), ("PT", 1, 0), ("PT", 2, 0), ("DN", 0), ("PT", 3, 0),
        ("T2", 1), ("PT", 4, 0), ("A", 0), ("PT", 4, 1), ("FC", 1, 0), ("PT", 5, 0), ("FC", 1, 1),
        ("PT", 5, 1), ("FC", 1, 2), ("PT", 6, 0), ("OT", 0), ("FC", 1, 3), ("PT", 6, 1), ("O", 0),
        ("PT", 7, 0), ("PT", 7, 1), ("DN", 1), ("T1", 0), ("T1", 1), ("A", 1), ("T2", 0), ("OT", 1),
        ("O", 1),
    ]
    pt_slots = [(t, h) for t in range(NT) for h in range(t // G + 1)]
    FIRST_ORDER = [
        ("QK", "q", 0), ("ROWS", 0, 0), ("ROWS", 0, 1), ("QK", "k", 0), ("ROWS", 1, 0), ("ROWS", 1, 1),
        ("QK", "q", 1), ("QK", "k", 1), ("PT", 0, 0), ("PT", 1, 0), ("PT", 2, 0), ("PT", 3, 0),
        ("PT", 4, 0), ("PT", 4, 1), ("A", 0), ("PT", 5, 0), ("PT", 5, 1), ("PT", 6, 0), ("PT", 6, 1),
        ("O", 0), ("PT", 7, 0), ("PT", 7, 1), ("T1", 0), ("T1", 1), ("A", 1), ("T2", 0), ("O", 1),
    ]
    LAST_ORDER = [
        ("FC", 0, 0), ("FC", 0, 1), ("FC", 0, 2), ("FC", 0, 3), ("T2", 1), ("DN", 0), ("FC", 1, 0),
        ("FC", 1, 1), ("FC", 1, 2), ("FC", 1, 3), ("DN", 1), ("OT", 0), ("OT", 1),
    ]
    NO_AHEAD_ORDER = [s for s in WORK_ORDER if s[0] != "T1"]
    BEFORE_LOOP = [("T1", g) for g in range(NG)]
    assert len(WORK_ORDER) % RING == 0
    PT_NO = {s: n for n, s in enumerate(pt_slots)}
    N_PT = len(PT_NO)

    def at(b, n):
        return isinstance(b, int) and b == n

    def order_of(b):
        return (FIRST_ORDER if at(b, 0) else NO_AHEAD_ORDER if at(b, B - 1) else
                LAST_ORDER if at(b, B) else WORK_ORDER)

    def place(b, step):
        i = order_of(b).index(step)
        if at(b, 0):
            before = bank = len(BEFORE_LOOP)
        elif at(b, B):
            before = bank = (len(BEFORE_LOOP) + len(FIRST_ORDER) + (B - 2) * len(WORK_ORDER)
                             + len(NO_AHEAD_ORDER))
        else:
            bank = len(BEFORE_LOOP) + len(FIRST_ORDER)
            before = (b - 1) * len(WORK_ORDER) + bank
        return before + i + 1, (bank + i) % RING

    ctx = ExitStack()
    with ctx:
        def sb(name, shape, dt=F32):
            return ctx.enter_context(nc.sbuf_tensor(name, shape, dt))

        def pb(name, shape):
            return ctx.enter_context(nc.psum_tensor(name, shape, F32))

        def sem(name):
            return ctx.enter_context(nc.semaphore(name))

        ident = sb("ident", [P, P])
        ident16 = sb("ident16", [P, P], BF16)
        mask16 = sb("mask16", [P, P], BF16)
        minus_half = sb("minus_half", [P, G])
        ct_sb = sb("ct_sb", [P, B])
        silu_den = sb("silu_den", [P, B])
        silu_rec = sb("silu_rec", [P, B])
        silu = sb("silu", [P, B])
        wmod_sb = sb("wmod_sb", [P, 6 * D])
        wq_sb = sb("wq_sb", [P, D])
        wk_sb = sb("wk_sb", [P, D])
        wv_sb = sb("wv_sb", [P, D])
        wfc_sb = sb("wfc_sb", [P, F])
        wproj_sb = sb("wproj_sb", [P, NF, D])
        bq_sb = sb("bq_sb", [P, 1])
        bk_sb = sb("bk_sb", [P, 1])
        bv_sb = sb("bv_sb", [P, 1])
        wq_s = sb("wq_s", [P, D])
        bq_s = sb("bq_s", [P, 1])
        wq_h, wq_l = sb("wq_h", [P, D], F32R), sb("wq_l", [P, D], F32R)
        wk_h, wk_l = sb("wk_h", [P, D], F32R), sb("wk_l", [P, D], F32R)
        wfc_h, wfc_l = sb("wfc_h", [P, F], F32R), sb("wfc_l", [P, F], F32R)
        mod = sb("mod", [P, 6, B])
        CA, CB, SA, SB, GA, GB = range(6)
        gate_sign = sb("gate_sign", [P, 2, B])
        gate_size = sb("gate_size", [P, 2, B])
        bias_column = sb("bias_column", [P, B])
        ga_wide = sb("ga_wide", [P, B, P])
        bias_wide = sb("bias_wide", [P, B, P])
        wv_out = sb("wv_out", [P, B, D])
        ga_rows = sb("ga_rows", [P, B, D])
        wv_ga = sb("wv_ga", [P, B, D])
        bias_rows = sb("bias_rows", [P, B, D])

        x_in = sb("x_in", [P, NT, D])
        x_res = sb("x_res", [P, NT, D])
        z1 = sb("z1", [P, NT, D])
        z1_h, z1_l = sb("z1_h", [P, NT, D], F32R), sb("z1_l", [P, NT, D], F32R)
        h1 = sb("h1", [P, T])
        h1_h, h1_l = sb("h1_h", [P, T], F32R), sb("h1_l", [P, T], F32R)
        q_h, q_l = sb("q_h", [P, T], F32R), sb("q_l", [P, T], F32R)
        k_h, k_l = sb("k_h", [P, T], F32R), sb("k_l", [P, T], F32R)
        probs = sb("probs", [P, 2, T])
        NS = NT
        p_h, p_l = sb("p_h", [P, NS, W], F32R), sb("p_l", [P, NS, W], F32R)
        attended = sb("attended", [P, NG, W])
        x1 = sb("x1", [P, NT, D])
        z2 = sb("z2", [P, NT, D])
        h2 = sb("h2", [P, T])
        h2_h, h2_l = sb("h2_h", [P, T], F32R), sb("h2_l", [P, T], F32R)
        relu = sb("relu", [P, NF, W])
        act2 = sb("act2", [P, NF, W])
        current = sb("current", [P, NG, W])
        spikes = sb("spikes", [P, 2, W])
        spikes_g = sb("spikes_g", [P, 2, W])
        y_out = sb("y_out", [P, NG, G, D])
        neg_max = sb("neg_max", [P, NT])
        row_sum = sb("row_sum", [P, NT])
        row_rec = sb("row_rec", [P, NT])
        stats1, stats2 = sb("stats1", [P, NT, 6]), sb("stats2", [P, NT, 6])
        mv1, mv2 = sb("mv1", [P, NT, 2]), sb("mv2", [P, NT, 2])
        var1, var2 = sb("var1", [P, NT]), sb("var2", [P, NT])
        rstd1, rstd2 = sb("rstd1", [P, NT]), sb("rstd2", [P, NT])
        shift1, shift2 = sb("shift1", [P, NT]), sb("shift2", [P, NT])

        scores = pb("scores", [P, 2, T])
        work = pb("work", [P, RING, W])

        c_loaded, wmod_loaded = sem("c_loaded"), sem("wmod_loaded")
        qk_loaded, v_loaded, ffn_loaded = sem("qk_loaded"), sem("v_loaded"), sem("ffn_loaded")
        x_loaded = [sem(f"x_loaded{g}") for g in range(NG)]
        stored = [sem(f"stored{g}") for g in range(NG)]
        const_step = sem("const_step")
        silu_step = sem("silu_step")
        act_waited, dve_waited, pool_waited = sem("act_waited"), sem("dve_waited"), sem("pool_waited")
        mod_step = sem("mod_step")
        weight_step = sem("weight_step")
        wfc_step = sem("wfc_step")
        columns_ready = sem("columns_ready")
        wide_ready = sem("wide_ready")
        rows_copied = sem("rows_copied")
        wv_out_step = sem("wv_out_step")
        work_ready = sem("work_ready")
        scores_ready = sem("scores_ready")
        qk_high, qk_low = sem("qk_high"), sem("qk_low")
        probs_ready = sem("probs_ready")
        pt_high, pt_low = sem("pt_high"), sem("pt_low")
        attended_ready = sem("attended_ready")
        h1_full, h1_high, h1_low = sem("h1_full"), sem("h1_high"), sem("h1_low")
        h2_full, h2_high, h2_low = sem("h2_full"), sem("h2_high"), sem("h2_low")
        relu_ready, act2_ready = sem("relu_ready"), sem("act2_ready")
        current_ready = sem("current_ready")
        spike_step = sem("spike_step")
        spikes_scaled = sem("spikes_scaled")
        y_ready = sem("y_ready")
        max_ready = sem("max_ready")
        rec_ready = sem("rec_ready")
        x1_ready = sem("x1_ready")
        bn1, bn2 = sem("bn1"), sem("bn2")
        mv1_ready, mv2_ready = sem("mv1_ready"), sem("mv2_ready")
        rstd1_step, rstd2_step = sem("rstd1_step"), sem("rstd2_step")
        first_step = [sem(f"first_step{g}") for g in range(NG)]
        z1_ready, z2_ready = sem("z1_ready"), sem("z2_ready")
        z1_high, z1_low = sem("z1_high"), sem("z1_low")
        x_res_ready = sem("x_res_ready")

        block = ctx.enter_context(nc.Block())

        def cols(g):
            return slice(g * W, (g + 1) * W)

        def slot(g, kt):
            return kt + (NS - G * (g + 1))

        def halves(g, half):
            first = G * g + half * (G // 2)
            return range(first, first + G // 2)

        def plain(ap):
            return ap.bitcast(F32)

        @block.sync
        def _(sp):
            def load_x(src, g):
                rows = slice(g * G, (g + 1) * G)
                sp.dma_start(x_in[:, rows, :], src[:, rows, :]).then_inc(x_loaded[g], 16)

            load_x(x_v[0], 0)
            sp.dma_start(ct_sb[:, :], c_t).then_inc(c_loaded, 16)
            load_x(x_v[0], 1)
            sp.dma_start(wmod_sb[:, :], w_mod).then_inc(wmod_loaded, 16)
            for dst, src in ((wq_sb, wq_t), (wk_sb, wk_t), (bq_sb, bq), (bk_sb, bk)):
                sp.dma_start(dst[:, :], src).then_inc(qk_loaded, 16)
            sp.dma_start(wv_sb[:, :], wv_t).then_inc(v_loaded, 16)
            sp.dma_start(bv_sb[:, :], bv).then_inc(v_loaded, 16)
            sp.dma_start(wfc_sb[:, :], w_fc_t).then_inc(ffn_loaded, 16)
            sp.dma_start(wproj_sb[:, :, :], w_proj_t).then_inc(ffn_loaded, 16)

            def next_x(b, src):
                sp.wait_ge(x_res_ready, NG * b + NG)
                sp.wait_ge(z1_ready, NT * b + NT)
                for g in range(NG):
                    load_x(src, g)

            def store(f, g):
                sp.wait_ge(y_ready, NG * f + g + 1)
                sp.dma_start(out_v[f][:, g * G:(g + 1) * G, :], y_out[:, g, :, :]).then_inc(stored[g], 16)

            next_x(0, x_v[1])
            with sp.Fori(1, B - 1) as b:
                next_x(b, x_v[b + 1])
                for g in range(NG):
                    store(b - 1, g)
            for f in (B - 2, B - 1):
                for g in range(NG):
                    store(f, g)
            for g in range(NG):
                sp.wait_ge(stored[g], 16 * B)
            for g in range(NG):
                sp.wait_ge(x_loaded[g], 16 * B)

        @block.tensor
        def _(pe):
            mm = nc.tensor.matmul

            def three(dst, a_h, a_l, b_h, b_l, start=True, stop=True):
                mm(dst, a_h, b_h, start=start, stop=False)
                mm(dst, a_l, b_h, start=False, stop=False)
                return mm(dst, a_h, b_l, start=False, stop=stop)

            def bank_reader(b, step):
                kind, rest = step[0], step[1:]
                if kind == "QK":
                    return qk_low, 2 * NG * b + 2 * rest[1] + (rest[0] == "k") + 1
                if kind == "PT":
                    return pt_low, N_PT * b + PT_NO[rest] + 1
                if kind == "ROWS":
                    return rows_copied, 2 * rest[0] + rest[1] + 1
                if kind == "A":
                    return attended_ready, NG * b + rest[0] + 1
                if kind == "O":
                    return x1_ready, NT * b + G * (rest[0] + 1)
                if kind == "T1":
                    return h1_full, NG * (b + 1) + rest[0] + 1
                if kind == "T2":
                    return h2_full, NG * (b - rest[0]) + rest[0] + 1
                if kind == "FC":
                    return relu_ready, NG * NF * (b - 1) + NF * rest[0] + rest[1] + 1
                if kind == "DN":
                    return current_ready, NG * (b - 1) + rest[0] + 1
                return y_ready, NG * (b - 1) + rest[0] + 1

            def work_tile(b, step):
                i = order_of(b).index(step)
                if i >= RING:
                    pe.wait_ge(*bank_reader(b, order_of(b)[i - RING]))
                elif at(b, 0):
                    if i >= RING - len(BEFORE_LOOP):
                        pe.wait_ge(*bank_reader(-1, BEFORE_LOOP[i - RING]))
                else:
                    last = FIRST_ORDER if at(b, 1) else NO_AHEAD_ORDER if at(b, B) else WORK_ORDER
                    pe.wait_ge(*bank_reader(b - 1, last[i - RING]))
                return work[:, place(b, step)[1], :]

            def rows_to_columns(dst, src, g):
                for i in range(G):
                    last = nc.tensor.transpose(dst[:, i * P:(i + 1) * P], src[:, g * G + i, :], ident[:, :])
                return last

            def t1(n, g, dst):
                pe.wait_ge(z1_ready, NT * n + G * (g + 1))
                rows_to_columns(dst, z1, g).then_inc(work_ready, 1)

            pe.wait_ge(const_step, 6)
            for _ in range(WARM_UP):
                mm(work[:, 0, 0:P], ident[:, :], ident[:, :], start=True, stop=True)
            pe.wait_ge(silu_step, 4)
            pe.wait_ge(wmod_loaded, 16)
            for n, j in enumerate((SCALEA, SCALEB, SHIFTA, SHIFTB, GATEA, GATEB)):
                mm(scores[:, 0, n * B:(n + 1) * B], wmod_sb[:, j * D:(j + 1) * D], silu[:, :],
                   start=True, stop=True).then_inc(columns_ready, 1)
            t1(0, 0, work[:, 0, :])
            pe.wait_ge(mod_step, 2)
            pe.wait_ge(v_loaded, 2 * 16)
            mm(scores[:, 0, W:W + B], wv_sb[:, :], mod[:, SA, 0:B],
               start=True, stop=True).then_inc(columns_ready, 1)
            t1(0, 1, work[:, 1, :])
            pe.wait_ge(weight_step, 6)

            def to_rows(b, n, half):
                dst = work_tile(b, ("ROWS", n, half))
                wide = (ga_wide, bias_wide)[n]
                pe.wait_ge(wide_ready, n + 1)
                for i in range(G):
                    last = nc.tensor.transpose(dst[:, i * P:(i + 1) * P], wide[:, half * G + i, :], ident[:, :])
                last.then_inc(work_ready, 1)

            def qk(b, which, g):
                w_h, w_l = (wq_h, wq_l) if which == "q" else (wk_h, wk_l)
                dst = work_tile(b, ("QK", which, g))
                pe.wait_ge(h1_high, NG * b + g + 1)
                pe.wait_ge(h1_low, NG * b + g + 1)
                three(dst, w_h[:, :], w_l[:, :], h1_h[:, cols(g)], h1_l[:, cols(g)]).then_inc(work_ready, 1)

            def score(b, t):
                g = t // G
                pe.wait_ge(qk_low, 2 * NG * b + 2 * g + 2)
                if not (at(b, 0) and t < 2):
                    pe.wait_ge(probs_ready, NT * b + t - 1)
                else:
                    pe.wait_ge(mod_step, 8)
                width = (t + 1) * P
                rows = slice(t * P, (t + 1) * P)
                for lo in range(0, width, W):
                    n = max(min(width - lo, W), 2 * P)
                    diagonal = lo + W >= width
                    three(scores[:, t % 2, lo:lo + n], q_h[:, rows], q_l[:, rows],
                          k_h[:, lo:lo + n], k_l[:, lo:lo + n], stop=not diagonal)
                last = mm(scores[:, t % 2, t * P:width], ident16[:, :], mask16[:, :],
                          start=False, stop=True)
                last.then_inc(scores_ready, 1)

            def transpose_probs(b, t, h):
                dst = work_tile(b, ("PT", t, h))
                pe.wait_ge(probs_ready, NT * b + t + 1)
                blocks = range(h * G, min(h * G + G, t + 1))
                for kt in blocks:
                    last = nc.tensor.transpose(dst[:, (kt - h * G) * P:(kt - h * G + 1) * P],
                                               probs[:, t % 2, kt * P:(kt + 1) * P], ident[:, :])
                last.then_inc(work_ready, 1)

            def attend(b, g):
                dst = work_tile(b, ("A", g))
                if at(b, 0):
                    pe.wait_ge(const_step, 8)
                pe.wait_ge(pt_low, N_PT * b + PT_NO[(G * g + G - 1, g)] + 1)
                pe.wait_ge(z1_low, NG * b + g + 1)
                last_kt = G * (g + 1) - 1
                for kt in range(last_kt + 1):
                    c0 = min(max(kt - G * g, 0) * P, W - 2 * P)
                    s = slot(g, kt)
                    last = three(dst[:, c0:W], z1_h[:, kt, :], z1_l[:, kt, :],
                                 p_h[:, s, c0:W], p_l[:, s, c0:W], start=kt == 0, stop=kt == last_kt)
                last.then_inc(work_ready, 1)

            def project_out(b, g):
                dst = work_tile(b, ("O", g))
                if at(b, 0):
                    pe.wait_ge(wv_out_step, 2)
                pe.wait_ge(attended_ready, NG * b + g + 1)
                for i in range(G):
                    last = mm(dst[:, i * P:(i + 1) * P], attended[:, g, i * P:(i + 1) * P],
                              wv_out[:, b, :], start=True, stop=True)
                last.then_inc(work_ready, 1)

            def t2(b, g):
                dst = work_tile(b, ("T2", g))
                pe.wait_ge(z2_ready, NT * (b - g) + G * (g + 1))
                rows_to_columns(dst, z2, g).then_inc(work_ready, 1)

            def up(b, c, j):
                dst = work_tile(b, ("FC", c, j))
                pe.wait_ge(h2_high, NG * (b - 1) + c + 1)
                pe.wait_ge(h2_low, NG * (b - 1) + c + 1)
                w = slice(j * P, (j + 1) * P)
                three(dst, wfc_h[:, w], wfc_l[:, w], h2_h[:, cols(c)], h2_l[:, cols(c)])\
                    .then_inc(work_ready, 1)

            def down(b, c):
                dst = work_tile(b, ("DN", c))
                for j in range(NF):
                    pe.wait_ge(act2_ready, NG * NF * (b - 1) + NF * c + j + 1)
                    last = mm(dst, wproj_sb[:, j, :], act2[:, j, :], start=j == 0, stop=j == NF - 1)
                last.then_inc(work_ready, 1)

            def spikes_back(b, c):
                dst = work_tile(b, ("OT", c))
                pe.wait_ge(spikes_scaled, NG * (b - 1) + c + 1)
                for i in range(G):
                    last = nc.tensor.transpose(dst[:, i * P:(i + 1) * P],
                                               spikes_g[:, c, i * P:(i + 1) * P], ident[:, :])
                last.then_inc(work_ready, 1)

            def first_attention(b):
                qk(b, "q", 0)
                to_rows(b, 0, 0)
                to_rows(b, 0, 1)
                qk(b, "k", 0)
                to_rows(b, 1, 0)
                to_rows(b, 1, 1)
                qk(b, "q", 1)
                score(b, 0)
                score(b, 1)
                qk(b, "k", 1)
                score(b, 2)
                transpose_probs(b, 0, 0)
                score(b, 3)
                transpose_probs(b, 1, 0)
                score(b, 4)
                transpose_probs(b, 2, 0)
                score(b, 5)
                transpose_probs(b, 3, 0)
                score(b, 6)
                transpose_probs(b, 4, 0)
                transpose_probs(b, 4, 1)
                attend(b, 0)
                transpose_probs(b, 5, 0)
                transpose_probs(b, 5, 1)
                score(b, 7)
                transpose_probs(b, 6, 0)
                transpose_probs(b, 6, 1)
                project_out(b, 0)
                transpose_probs(b, 7, 0)
                transpose_probs(b, 7, 1)
                t1(b + 1, 0, work_tile(b, ("T1", 0)))
                t1(b + 1, 1, work_tile(b, ("T1", 1)))
                attend(b, 1)
                t2(b, 0)
                project_out(b, 1)

            def iteration(b, look_ahead=True):
                qk(b, "q", 0)
                qk(b, "k", 0)
                qk(b, "q", 1)
                up(b, 0, 0)
                qk(b, "k", 1)
                score(b, 0)
                score(b, 1)
                up(b, 0, 1)
                up(b, 0, 2)
                score(b, 2)
                transpose_probs(b, 0, 0)
                up(b, 0, 3)
                transpose_probs(b, 1, 0)
                score(b, 3)
                score(b, 4)
                transpose_probs(b, 2, 0)
                down(b, 0)
                score(b, 5)
                transpose_probs(b, 3, 0)
                t2(b, 1)
                score(b, 6)
                transpose_probs(b, 4, 0)
                attend(b, 0)
                transpose_probs(b, 4, 1)
                up(b, 1, 0)
                transpose_probs(b, 5, 0)
                up(b, 1, 1)
                score(b, 7)
                transpose_probs(b, 5, 1)
                up(b, 1, 2)
                transpose_probs(b, 6, 0)
                spikes_back(b, 0)
                up(b, 1, 3)
                transpose_probs(b, 6, 1)
                project_out(b, 0)
                transpose_probs(b, 7, 0)
                transpose_probs(b, 7, 1)
                down(b, 1)
                if look_ahead:
                    t1(b + 1, 0, work_tile(b, ("T1", 0)))
                    t1(b + 1, 1, work_tile(b, ("T1", 1)))
                attend(b, 1)
                t2(b, 0)
                spikes_back(b, 1)
                project_out(b, 1)

            def last_feed_forward(b):
                up(b, 0, 0)
                up(b, 0, 1)
                up(b, 0, 2)
                up(b, 0, 3)
                t2(b, 1)
                down(b, 0)
                up(b, 1, 0)
                up(b, 1, 1)
                up(b, 1, 2)
                up(b, 1, 3)
                down(b, 1)
                spikes_back(b, 0)
                spikes_back(b, 1)

            first_attention(0)
            pe.wait_ge(wfc_step, 2)
            pe.wait_ge(ffn_loaded, 2 * 16)
            iteration(1)
            with pe.Fori(2, B - 1) as b:
                iteration(b)
            iteration(B - 1, look_ahead=False)
            last_feed_forward(B)

        @block.scalar
        def _(act):
            act.wait_ge(c_loaded, 16)
            nc.scalar.activation(silu_den[:, :], ct_sb[:, :], ACT.Exp, scale=-1.0).then_inc(silu_step, 1)

            def ready(b, step):
                count, bank = place(b, step)
                act.wait_ge(work_ready, count)
                return work[:, bank, :]

            def waited():
                act.sem_inc(act_waited, 1)

            def qk_h(b, which, g):
                src = ready(b, ("QK", which, g))
                if g == 0 and which == "q" and not at(b, 0):
                    act.wait_ge(scores_ready, NT * b)
                dst, bias = (q_h, bq_s) if which == "q" else (k_h, bk_sb)
                nc.scalar.activation(dst[:, cols(g)], src, ACT.Identity, bias=bias[:, 0:1]).then_inc(qk_high, 1)

            def exponential(b, t):
                n = NT * b + t
                act.wait_ge(max_ready, n + 1)
                if t >= 2:
                    act.wait_ge(work_ready, place(b, ("PT", t - 2, (t - 2) // G))[0])
                elif not at(b, 0):
                    act.wait_ge(rec_ready, NG * b)
                width = (t + 1) * P
                nc.scalar.activation(probs[:, t % 2, 0:width], scores[:, t % 2, 0:width], ACT.Exp,
                                     bias=neg_max[:, t:t + 1],
                                     accum_out=row_sum[:, t:t + 1]).then_inc(probs_ready, 1)

            def pt_h(b, t, h):
                src = ready(b, ("PT", t, h))
                g, n = t // G, min(G, t + 1 - h * G)
                if (t, h) == (G, 1):
                    act.wait_ge(work_ready, place(b, ("A", 0))[0])
                elif t == 0 and not at(b, 0):
                    act.wait_ge(work_ready, place(0 if at(b, 1) else b - 1, ("A", 1))[0])
                s = slot(g, h * G)
                nc.scalar.activation(p_h[:, s:s + n, (t % G) * P:(t % G + 1) * P],
                                     src[:, 0:n * P].rearrange("p (k q) -> p k q", q=P),
                                     ACT.Copy).then_inc(pt_high, 1)

            def copy_attended(b, g):
                nc.scalar.activation(attended[:, g, :], ready(b, ("A", g)),
                                     ACT.Copy).then_inc(attended_ready, 1)

            def copy_current(b, c):
                src = ready(b, ("DN", c))
                if not at(b, 1):
                    act.wait_ge(spike_step, NUM_STEPS * (NG * (b - 2) + c + 1))
                nc.scalar.activation(current[:, c, :], src, ACT.Copy).then_inc(current_ready, 1)

            def modulate1(n, src, g):
                if not at(n, 0):
                    act.wait_ge(h1_low, NG * (n - 1) + g + 1)
                waited()
                nc.scalar.activation(h1[:, cols(g)], src, ACT.Identity, bias=mod[:, SA, bass.ds(n, 1)],
                                     scale=mod[:, CA, bass.ds(n, 1)]).then_inc(h1_full, 1)

            def modulate2(b, g):
                src = ready(b, ("T2", g))
                n = b - g
                if not at(n, 0):
                    act.wait_ge(h2_low, NG * (n - 1) + g + 1)
                waited()
                nc.scalar.activation(h2[:, cols(g)], src, ACT.Identity, bias=mod[:, SB, bass.ds(n, 1)],
                                     scale=mod[:, CB, bass.ds(n, 1)]).then_inc(h2_full, 1)

            def rectify(b, c, j):
                src = ready(b, ("FC", c, j))
                if not (at(b, 1) and c == 0):
                    act.wait_ge(act2_ready, NF * (NG * (b - 1) + c - 1) + j + 1)
                nc.scalar.activation(relu[:, j, :], src, ACT.Relu).then_inc(relu_ready, 1)

            def scale_spikes(b, c):
                f = b - 1
                act.wait_ge(spike_step, NUM_STEPS * (NG * f + c + 1))
                waited()
                nc.scalar.activation(spikes_g[:, c, :], spikes[:, c, :], ACT.Identity,
                                     scale=mod[:, GB, bass.ds(f, 1)]).then_inc(spikes_scaled, 1)

            def normalise(src, z, rstd, shift, step, ready_, n, g, half, skipped=0):
                if half == 0:
                    act.wait_ge(step, 4 * (NG * n + g - skipped) + 4)
                for i in halves(g, half):
                    nc.scalar.activation(z[:, i, :], src[:, i, :], ACT.Identity, bias=shift[:, i:i + 1],
                                         scale=rstd[:, i:i + 1]).then_inc(ready_, 1)

            def normalise1(n, g, half):
                if half == 0 and not at(n, 0):
                    act.wait_ge(z1_low, NG * (n - 1) + g + 1)
                normalise(x_in, z1, rstd1, shift1, rstd1_step, z1_ready, n, g, half, skipped=NG)

            def normalise2(n, g, half):
                normalise(x1, z2, rstd2, shift2, rstd2_step, z2_ready, n, g, half)

            def copy_rows(b, n, half):
                batches = slice(half * G, half * G + G)
                nc.scalar.activation((ga_rows, bias_rows)[n][:, batches, :].rearrange("p b d -> p (b d)"),
                                     ready(b, ("ROWS", n, half)), ACT.Copy).then_inc(rows_copied, 1)

            def widen(wide, column):
                nc.scalar.activation(wide[:, :, :], column.unsqueeze(2).to_broadcast([P, B, P]),
                                     ACT.Copy).then_inc(wide_ready, 1)

            def modulate_first(g):
                act.wait_ge(work_ready, g + 1)
                modulate1(0, work[:, g, :], g)

            act.wait_ge(qk_loaded, 4 * 16)
            nc.scalar.activation(wq_s[:, :], wq_sb[:, :], ACT.Copy, scale=QK_SCALE).then_inc(weight_step, 1)
            nc.scalar.activation(bq_s[:, :], bq_sb[:, :], ACT.Copy, scale=QK_SCALE).then_inc(weight_step, 1)
            nc.scalar.activation(wk_h[:, :], wk_sb[:, :], ACT.Copy).then_inc(weight_step, 1)
            act.wait_ge(weight_step, 3)
            nc.scalar.activation(wq_h[:, :], wq_s[:, :], ACT.Copy).then_inc(weight_step, 1)
            act.wait_ge(mod_step, 2)
            modulate_first(0)
            act.wait_ge(mod_step, 6)
            widen(ga_wide, mod[:, GA, 0:B])
            act.wait_ge(mod_step, 8)
            widen(bias_wide, bias_column[:, :])
            modulate_first(1)

            def first_attention(b):
                qk_h(b, "q", 0)
                copy_rows(b, 0, 0)
                copy_rows(b, 0, 1)
                qk_h(b, "k", 0)
                copy_rows(b, 1, 0)
                copy_rows(b, 1, 1)
                qk_h(b, "q", 1)
                exponential(b, 0)
                exponential(b, 1)
                qk_h(b, "k", 1)
                pt_h(b, 0, 0)
                exponential(b, 2)
                pt_h(b, 1, 0)
                exponential(b, 3)
                pt_h(b, 2, 0)
                exponential(b, 4)
                pt_h(b, 3, 0)
                exponential(b, 5)
                pt_h(b, 4, 0)
                exponential(b, 6)
                pt_h(b, 4, 1)
                copy_attended(b, 0)
                pt_h(b, 5, 0)
                pt_h(b, 5, 1)
                normalise1(b + 1, 0, 0)
                normalise1(b + 1, 0, 1)
                pt_h(b, 6, 0)
                exponential(b, 7)
                pt_h(b, 6, 1)
                normalise1(b + 1, 1, 0)
                pt_h(b, 7, 0)
                pt_h(b, 7, 1)
                normalise1(b + 1, 1, 1)
                modulate1(b + 1, ready(b, ("T1", 0)), 0)
                modulate1(b + 1, ready(b, ("T1", 1)), 1)
                normalise2(b, 0, 0)
                normalise2(b, 0, 1)
                copy_attended(b, 1)
                modulate2(b, 0)

            def iteration(b, look_ahead=True):
                qk_h(b, "q", 0)
                qk_h(b, "k", 0)
                qk_h(b, "q", 1)
                rectify(b, 0, 0)
                qk_h(b, "k", 1)
                exponential(b, 0)
                rectify(b, 0, 1)
                exponential(b, 1)
                rectify(b, 0, 2)
                exponential(b, 2)
                pt_h(b, 0, 0)
                exponential(b, 3)
                rectify(b, 0, 3)
                pt_h(b, 1, 0)
                normalise2(b - 1, 1, 0)
                pt_h(b, 2, 0)
                exponential(b, 4)
                normalise2(b - 1, 1, 1)
                copy_current(b, 0)
                pt_h(b, 3, 0)
                modulate2(b, 1)
                exponential(b, 5)
                pt_h(b, 4, 0)
                if look_ahead:
                    normalise1(b + 1, 0, 0)
                copy_attended(b, 0)
                exponential(b, 6)
                pt_h(b, 4, 1)
                pt_h(b, 5, 0)
                rectify(b, 1, 0)
                scale_spikes(b, 0)
                rectify(b, 1, 1)
                pt_h(b, 5, 1)
                rectify(b, 1, 2)
                pt_h(b, 6, 0)
                exponential(b, 7)
                pt_h(b, 6, 1)
                rectify(b, 1, 3)
                pt_h(b, 7, 0)
                if look_ahead:
                    normalise1(b + 1, 0, 1)
                    normalise1(b + 1, 1, 0)
                pt_h(b, 7, 1)
                if look_ahead:
                    normalise1(b + 1, 1, 1)
                copy_current(b, 1)
                if look_ahead:
                    modulate1(b + 1, ready(b, ("T1", 0)), 0)
                normalise2(b, 0, 0)
                if look_ahead:
                    modulate1(b + 1, ready(b, ("T1", 1)), 1)
                normalise2(b, 0, 1)
                scale_spikes(b, 1)
                copy_attended(b, 1)
                modulate2(b, 0)

            def last_feed_forward(b):
                rectify(b, 0, 0)
                rectify(b, 0, 1)
                rectify(b, 0, 2)
                rectify(b, 0, 3)
                modulate2(b, 1)
                copy_current(b, 0)
                rectify(b, 1, 0)
                rectify(b, 1, 1)
                rectify(b, 1, 2)
                rectify(b, 1, 3)
                copy_current(b, 1)
                scale_spikes(b, 0)
                scale_spikes(b, 1)

            first_attention(0)
            iteration(1)
            with act.Fori(2, B - 1) as b:
                iteration(b)
            iteration(B - 1, look_ahead=False)
            last_feed_forward(B)

        @block.vector
        def _(dve):
            v = nc.vector
            def waited():
                dve.sem_inc(dve_waited, 1)

            def statistics(src, stats, counted, g, half):
                for i in halves(g, half):
                    v.bn_stats(stats[:, i, :], src[:, i, :]).then_inc(counted, 1)

            def aggregate(stats, mv, counted, ready_, n, g):
                dve.wait_ge(counted, NT * n + G * (g + 1))
                waited()
                for i in range(G * g, G * g + G):
                    v.bn_aggr(mv[:, i, :], stats[:, i, :]).then_inc(ready_, 1)

            def statistics1(n, g, half):
                if half == 0:
                    dve.wait_ge(x_loaded[g], 16 * (n + 1))
                    if not at(n, 0):
                        dve.wait_ge(z1_ready, NT * (n - 1) + G * (g + 1))
                statistics(x_in, stats1, bn1, g, half)

            def aggregate1(n, g):
                aggregate(stats1, mv1, bn1, mv1_ready, n, g)

            def statistics2(n, g, half):
                if half == 0:
                    dve.wait_ge(x1_ready, NT * n + G * (g + 1))
                    if not at(n, 0):
                        dve.wait_ge(z2_ready, NT * (n - 1) + G * (g + 1))
                statistics(x1, stats2, bn2, g, half)

            def aggregate2(n, g):
                aggregate(stats2, mv2, bn2, mv2_ready, n, g)

            def work_bank(b, step):
                return work[:, place(b, step)[1], :]

            def qk_l(b, which, g):
                n = 2 * NG * b + 2 * g + (which == "k")
                dve.wait_ge(qk_high, n + 1)
                high, low, bias = (q_h, q_l, bq_s) if which == "q" else (k_h, k_l, bk_sb)
                v.scalar_tensor_tensor(low[:, cols(g)], work_bank(b, ("QK", which, g)), bias[:, 0:1],
                                       plain(high[:, cols(g)]), ALU.add, ALU.subtract).then_inc(qk_low, 1)

            def maximum(b, t):
                dve.wait_ge(scores_ready, NT * b + t + 1)
                v.reduce_max(neg_max[:, t:t + 1], scores[:, t % 2, 0:(t + 1) * P], AX.X,
                             negate=True).then_inc(max_ready, 1)

            def pt_l(b, t, h):
                dve.wait_ge(pt_high, N_PT * b + PT_NO[(t, h)] + 1)
                g, n = t // G, min(G, t + 1 - h * G)
                s = slot(g, h * G)
                q = slice((t % G) * P, (t % G + 1) * P)
                src = work_bank(b, ("PT", t, h))[:, 0:n * P].rearrange("p (k q) -> p k q", q=P)
                v.tensor_tensor(p_l[:, s:s + n, q], src, plain(p_h[:, s:s + n, q]),
                                ALU.subtract).then_inc(pt_low, 1)

            def h2_high_part(n, g):
                dve.wait_ge(h2_full, NG * n + g + 1)
                v.tensor_copy(h2_h[:, cols(g)], h2[:, cols(g)]).then_inc(h2_high, 1)

            def h1_high_part(n, g):
                dve.wait_ge(h1_full, NG * n + g + 1)
                v.tensor_copy(h1_h[:, cols(g)], h1[:, cols(g)]).then_inc(h1_high, 1)

            def h1_low_part(n, g):
                dve.wait_ge(h1_high, NG * n + g + 1)
                v.tensor_tensor(h1_l[:, cols(g)], h1[:, cols(g)], plain(h1_h[:, cols(g)]),
                                ALU.subtract).then_inc(h1_low, 1)

            def h2_low_part(n, g):
                dve.wait_ge(h2_high, NG * n + g + 1)
                v.tensor_tensor(h2_l[:, cols(g)], h2[:, cols(g)], plain(h2_h[:, cols(g)]),
                                ALU.subtract).then_inc(h2_low, 1)

            def square(b, c, j):
                dve.wait_ge(relu_ready, NF * (NG * (b - 1) + c) + j + 1)
                if c > 0:
                    dve.wait_ge(work_ready, place(b, ("DN", c - 1))[0])
                v.tensor_tensor(act2[:, j, :], relu[:, j, :], relu[:, j, :], ALU.mult).then_inc(act2_ready, 1)

            def normalise2(n, g, half):
                if half == 0:
                    dve.wait_ge(rstd2_step, 4 * (NG * n + g) + 4)
                for i in halves(g, half):
                    v.tensor_scalar(z2[:, i, :], x1[:, i, :], rstd2[:, i:i + 1], shift2[:, i:i + 1],
                                    ALU.mult, ALU.add).then_inc(z2_ready, 1)

            def split_z1_high(b, g):
                own = slice(G * g, G * g + G)
                if not at(b, 0):
                    dve.wait_ge(work_ready, place(0 if at(b, 1) else b - 1, ("A", NG - 1))[0])
                dve.wait_ge(z1_ready, NT * b + G * (g + 1))
                v.tensor_copy(z1_h[:, own, :], z1[:, own, :]).then_inc(z1_high, 1)

            def invert_sums(b, g):
                dve.wait_ge(probs_ready, NT * b + G * (g + 1))
                if not at(b, 0):
                    dve.wait_ge(x1_ready, NT * (b - 1) + G * (g + 1))
                v.reciprocal(row_rec[:, G * g:G * g + G], row_sum[:, G * g:G * g + G]).then_inc(rec_ready, 1)

            def first_residual(b, g, half):
                count, bank = place(b, ("O", g))
                if half == 0:
                    dve.wait_ge(work_ready, count)
                    dve.wait_ge(rec_ready, NG * b + g + 1)
                    dve.wait_ge(x_res_ready, NG * b + g + 1)
                    if not at(b, 0):
                        dve.wait_ge(z2_ready, NT * (b - 1) + G * (g + 1))
                        dve.wait_ge(y_ready, NG * (b - 1) + g + 1)
                for t in halves(g, half):
                    i = t - G * g
                    v.scalar_tensor_tensor(x1[:, t, :], work[:, bank, i * P:(i + 1) * P],
                                           row_rec[:, t:t + 1], x_res[:, t, :],
                                           ALU.mult, ALU.add).then_inc(x1_ready, 1)

            def count_spikes(b, c, n):
                f = b - 1
                step = NUM_STEPS * (NG * f + c) + n
                if n == 0:
                    dve.wait_ge(current_ready, NG * f + c + 1)
                    if not at(b, 1):
                        dve.wait_ge(spikes_scaled, NG * (f - 1) + c + 1)
                    v.tensor_scalar(spikes[:, c, :], current[:, c, :], thetas[0], None, ALU.is_gt)\
                        .then_inc(spike_step, 1)
                else:
                    dve.wait_ge(spike_step, step)
                    v.scalar_tensor_tensor(spikes[:, c, :], current[:, c, :], thetas[n], spikes[:, c, :],
                                           ALU.is_gt, ALU.add).then_inc(spike_step, 1)

            def second_residual(b, c):
                f = b - 1
                count, bank = place(b, ("OT", c))
                dve.wait_ge(work_ready, count)
                if not at(b, 1):
                    dve.wait_ge(stored[c], 16 * f)
                v.tensor_tensor(y_out[:, c, :, :], work[:, bank, :].rearrange("p (t d) -> p t d", d=D),
                                x1[:, G * c:G * c + G, :], ALU.add).then_inc(y_ready, 1)

            def first_variance(g):
                for half in range(2):
                    statistics1(0, g, half)
                aggregate1(0, g)
                dve.wait_ge(mv1_ready, G * (g + 1))
                own = slice(G * g, G * g + G)
                v.tensor_scalar_add(var1[:, own], mv1[:, own, 1], LN_EPS).then_inc(first_step[g], 1)

            def first_shift(g):
                own = slice(G * g, G * g + G)
                dve.wait_ge(first_step[g], 2)
                v.scalar_tensor_tensor(shift1[:, own], mv1[:, own, 0], -1.0, rstd1[:, own],
                                       ALU.mult, ALU.mult).then_inc(first_step[g], 1)
                dve.wait_ge(first_step[g], 3)

            def first_normalise(i):
                v.tensor_scalar(z1[:, i, :], x_in[:, i, :], rstd1[:, i:i + 1], shift1[:, i:i + 1],
                                ALU.mult, ALU.add).then_inc(z1_ready, 1)

            dve.wait_ge(silu_step, 1)
            v.tensor_scalar_add(silu_rec[:, :], silu_den[:, :], 1.0).then_inc(silu_step, 1)
            dve.wait_ge(silu_step, 2)
            v.reciprocal(silu_den[:, :], silu_rec[:, :]).then_inc(silu_step, 1)
            dve.wait_ge(silu_step, 3)
            v.tensor_tensor(silu[:, :], ct_sb[:, :], silu_den[:, :], ALU.mult).then_inc(silu_step, 1)

            first_variance(0)
            first_variance(1)
            first_shift(0)
            for i in range(G):
                first_normalise(i)

            raw = scores[:, 0, 0:6 * B].rearrange("p (n b) -> p n b", b=B)
            dve.wait_ge(columns_ready, 6)
            v.tensor_scalar_add(mod[:, CA:CB + 1, 0:B], raw[:, CA:CB + 1, :], 1.0).then_inc(mod_step, 1)
            v.tensor_copy(mod[:, SA:SB + 1, 0:B], raw[:, SA:SB + 1, :]).then_inc(mod_step, 1)
            first_shift(1)
            gates = raw[:, GA:GB + 1, :]
            v.tensor_scalar(gate_sign[:, :, :], gates, 0.0, 2.0, ALU.is_ge, ALU.mult).then_inc(mod_step, 1)
            v.tensor_scalar(gate_size[:, :, :], gates, GATE_MIN, None, ALU.max).then_inc(mod_step, 1)
            first_normalise(G)
            dve.wait_ge(mod_step, 4)
            v.scalar_tensor_tensor(gate_size[:, :, :], gates, -1.0, gate_size[:, :, :],
                                   ALU.mult, ALU.max).then_inc(mod_step, 1)
            first_normalise(G + 1)
            dve.wait_ge(mod_step, 5)
            v.scalar_tensor_tensor(mod[:, GA:GB + 1, 0:B], gate_sign[:, :, :], 1.0, gate_size[:, :, :],
                                   ALU.subtract, ALU.mult).then_inc(mod_step, 1)
            first_normalise(G + 2)
            dve.wait_ge(mod_step, 6)
            v.tensor_scalar(mod[:, GB, 0:B], mod[:, GB, 0:B], 1.0 / NUM_STEPS, None, ALU.mult)\
                .then_inc(mod_step, 1)
            first_normalise(G + 3)
            dve.wait_ge(columns_ready, 7)
            v.scalar_tensor_tensor(bias_column[:, :], scores[:, 0, W:W + B], bv_sb[:, 0:1],
                                   mod[:, GA, 0:B], ALU.add, ALU.mult).then_inc(mod_step, 1)

            h1_high_part(0, 0)
            h1_low_part(0, 0)
            h1_high_part(0, 1)
            h1_low_part(0, 1)

            def first_attention(b):
                qk_l(b, "q", 0)
                split_z1_high(b, 0)
                qk_l(b, "k", 0)
                maximum(b, 0)
                split_z1_high(b, 1)
                maximum(b, 1)
                qk_l(b, "q", 1)
                maximum(b, 2)
                qk_l(b, "k", 1)
                maximum(b, 3)
                pt_l(b, 0, 0)
                pt_l(b, 1, 0)
                maximum(b, 4)
                pt_l(b, 2, 0)
                maximum(b, 5)
                statistics1(b + 1, 0, 0)
                pt_l(b, 3, 0)
                statistics1(b + 1, 0, 1)
                maximum(b, 6)
                aggregate1(b + 1, 0)
                pt_l(b, 4, 0)
                statistics1(b + 1, 1, 0)
                statistics1(b + 1, 1, 1)
                pt_l(b, 4, 1)
                aggregate1(b + 1, 1)
                maximum(b, 7)
                pt_l(b, 5, 0)
                pt_l(b, 5, 1)
                pt_l(b, 6, 0)
                invert_sums(b, 0)
                first_residual(b, 0, 0)
                pt_l(b, 6, 1)
                first_residual(b, 0, 1)
                pt_l(b, 7, 0)
                pt_l(b, 7, 1)
                statistics2(b, 0, 0)
                statistics2(b, 0, 1)
                aggregate2(b, 0)
                h1_high_part(b + 1, 0)
                h1_high_part(b + 1, 1)
                invert_sums(b, 1)
                h2_high_part(b, 0)
                first_residual(b, 1, 0)
                first_residual(b, 1, 1)

            def iteration(b, look_ahead=True):
                qk_l(b, "q", 0)
                qk_l(b, "k", 0)
                qk_l(b, "q", 1)
                statistics2(b - 1, 1, 0)
                maximum(b, 0)
                qk_l(b, "k", 1)
                maximum(b, 1)
                statistics2(b - 1, 1, 1)
                maximum(b, 2)
                split_z1_high(b, 0)
                aggregate2(b - 1, 1)
                maximum(b, 3)
                pt_l(b, 0, 0)
                maximum(b, 4)
                if look_ahead:
                    statistics1(b + 1, 0, 0)
                    statistics1(b + 1, 0, 1)
                split_z1_high(b, 1)
                if look_ahead:
                    statistics1(b + 1, 1, 0)
                    aggregate1(b + 1, 0)
                pt_l(b, 1, 0)
                if look_ahead:
                    statistics1(b + 1, 1, 1)
                pt_l(b, 2, 0)
                if look_ahead:
                    aggregate1(b + 1, 1)
                maximum(b, 5)
                invert_sums(b, 0)
                count_spikes(b, 0, 0)
                pt_l(b, 3, 0)
                h2_high_part(b - 1, 1)
                count_spikes(b, 0, 1)
                maximum(b, 6)
                pt_l(b, 4, 0)
                count_spikes(b, 0, 2)
                count_spikes(b, 0, 3)
                count_spikes(b, 0, 4)
                pt_l(b, 4, 1)
                pt_l(b, 5, 0)
                maximum(b, 7)
                pt_l(b, 5, 1)
                pt_l(b, 6, 0)
                second_residual(b, 0)
                pt_l(b, 6, 1)
                invert_sums(b, 1)
                first_residual(b, 0, 0)
                first_residual(b, 0, 1)
                pt_l(b, 7, 0)
                statistics2(b, 0, 0)
                pt_l(b, 7, 1)
                statistics2(b, 0, 1)
                aggregate2(b, 0)
                count_spikes(b, 1, 0)
                count_spikes(b, 1, 1)
                count_spikes(b, 1, 2)
                if look_ahead:
                    h1_high_part(b + 1, 0)
                count_spikes(b, 1, 3)
                count_spikes(b, 1, 4)
                if look_ahead:
                    h1_high_part(b + 1, 1)
                second_residual(b, 1)
                h2_high_part(b, 0)
                first_residual(b, 1, 0)
                first_residual(b, 1, 1)

            def last_feed_forward(b):
                statistics2(b - 1, 1, 0)
                statistics2(b - 1, 1, 1)
                aggregate2(b - 1, 1)
                square(b, 0, 0)
                normalise2(b - 1, 1, 0)
                normalise2(b - 1, 1, 1)
                square(b, 0, 1)
                square(b, 0, 2)
                h2_high_part(b - 1, 1)
                square(b, 0, 3)
                h2_low_part(b - 1, 1)
                count_spikes(b, 0, 0)
                square(b, 1, 0)
                square(b, 1, 1)
                count_spikes(b, 0, 1)
                square(b, 1, 2)
                square(b, 1, 3)
                count_spikes(b, 0, 2)
                count_spikes(b, 0, 3)
                count_spikes(b, 0, 4)
                count_spikes(b, 1, 0)
                count_spikes(b, 1, 1)
                count_spikes(b, 1, 2)
                count_spikes(b, 1, 3)
                count_spikes(b, 1, 4)
                second_residual(b, 0)
                second_residual(b, 1)

            first_attention(0)
            iteration(1)
            with dve.Fori(2, B - 1) as b:
                iteration(b)
            iteration(B - 1, look_ahead=False)
            last_feed_forward(B)

        @block.gpsimd
        def _(pool):
            g_ = nc.gpsimd
            g_.memset(ident[:, :], 0.0).then_inc(const_step, 1)
            g_.memset(mask16[:, :], 0.0).then_inc(const_step, 1)
            g_.memset(minus_half[:, :], -0.5).then_inc(const_step, 1)
            pool.wait_ge(const_step, 3)
            g_.affine_select(out=ident[:, :], in_=ident[:, :], compare_op=ALU.not_equal, fill=1.0,
                             base=0, pattern=[[-1, P]], channel_multiplier=1).then_inc(const_step, 1)
            g_.affine_select(out=mask16[:, :], in_=mask16[:, :], compare_op=ALU.is_ge, fill=MASKED,
                             base=0, pattern=[[-1, P]], channel_multiplier=1).then_inc(const_step, 1)
            pool.wait_ge(const_step, 5)
            g_.tensor_copy(ident16[:, :], ident[:, :]).then_inc(const_step, 1)
            zero = slice(W - 2 * P, W - P)
            for part in (p_h, p_l):
                g_.memset(plain(part[:, NS - 1, zero]), 0.0).then_inc(const_step, 1)

            def waited():
                pool.sem_inc(pool_waited, 1)

            def inverse_deviation(mv, var, rstd, shift, step, counted, n, g, skipped=0):
                pool.wait_ge(counted, NT * n + G * (g + 1))
                own = slice(G * g, G * g + G)
                waited()
                g_.tensor_scalar_add(var[:, own], mv[:, own, 1], LN_EPS).then_inc(step, 1)
                g_.tensor_scalar(shift[:, own], mv[:, own, 0], -1.0, None, ALU.mult).then_inc(step, 1)
                pool.wait_ge(step, 4 * (NG * n + g - skipped) + 2)
                g_.tensor_tensor(rstd[:, own], var[:, own], minus_half[:, :], ALU.pow).then_inc(step, 1)
                pool.wait_ge(step, 4 * (NG * n + g - skipped) + 3)
                g_.tensor_tensor(shift[:, own], shift[:, own], rstd[:, own], ALU.mult).then_inc(step, 1)

            def deviation1(n, g):
                inverse_deviation(mv1, var1, rstd1, shift1, rstd1_step, mv1_ready, n, g, skipped=NG)

            def deviation2(n, g):
                inverse_deviation(mv2, var2, rstd2, shift2, rstd2_step, mv2_ready, n, g)

            def h1_low_part(n, g):
                pool.wait_ge(h1_high, NG * n + g + 1)
                g_.tensor_tensor(h1_l[:, cols(g)], h1[:, cols(g)], plain(h1_h[:, cols(g)]),
                                 ALU.subtract).then_inc(h1_low, 1)

            def h2_low_part(n, g):
                pool.wait_ge(h2_high, NG * n + g + 1)
                g_.tensor_tensor(h2_l[:, cols(g)], h2[:, cols(g)], plain(h2_h[:, cols(g)]),
                                 ALU.subtract).then_inc(h2_low, 1)

            def split_z1_low(b, g):
                own = slice(G * g, G * g + G)
                pool.wait_ge(z1_high, NG * b + g + 1)
                g_.tensor_tensor(z1_l[:, own, :], z1[:, own, :], plain(z1_h[:, own, :]),
                                 ALU.subtract).then_inc(z1_low, 1)

            def add_bias_row(b, g):
                pool.wait_ge(x_loaded[g], 16 * (b + 1))
                if not at(b, 0):
                    pool.wait_ge(x1_ready, NT * (b - 1) + G * (g + 1))
                else:
                    pool.wait_ge(rows_copied, 4)
                waited()
                own = slice(G * g, G * g + G)
                row = bias_rows[:, b, :].unsqueeze(1).to_broadcast([P, G, D])
                g_.tensor_tensor(x_res[:, own, :], x_in[:, own, :], row, ALU.add).then_inc(x_res_ready, 1)

            def square(b, c, j):
                n = NG * NF * (b - 1) + NF * c + j
                pool.wait_ge(relu_ready, n + 1)
                if c > 0:
                    pool.wait_ge(work_ready, place(b, ("DN", c - 1))[0])
                elif not at(b, 1):
                    pool.wait_ge(work_ready, place(b - 1, ("DN", NG - 1))[0])
                g_.tensor_tensor(act2[:, j, :], relu[:, j, :], relu[:, j, :],
                                 ALU.mult).then_inc(act2_ready, 1)

            for g in range(NG):
                own = slice(G * g, G * g + G)
                pool.wait_ge(first_step[g], 1)
                g_.tensor_tensor(rstd1[:, own], var1[:, own], minus_half[:, :], ALU.pow)\
                    .then_inc(first_step[g], 1)
            pool.wait_ge(weight_step, 4)
            g_.tensor_tensor(wk_l[:, :], wk_sb[:, :], plain(wk_h[:, :]), ALU.subtract).then_inc(weight_step, 1)
            g_.tensor_tensor(wq_l[:, :], wq_s[:, :], plain(wq_h[:, :]), ALU.subtract).then_inc(weight_step, 1)

            def scale_wv():
                pool.wait_ge(v_loaded, 2 * 16)
                pool.wait_ge(rows_copied, 2)
                g_.tensor_tensor(wv_ga[:, :, :], ga_rows[:, :, :],
                                 wv_sb[:, :].unsqueeze(1).to_broadcast([P, B, D]), ALU.mult)\
                    .then_inc(wv_out_step, 1)
                pool.wait_ge(wv_out_step, 1)
                g_.tensor_tensor(wv_out[:, :, :], wv_ga[:, :, :],
                                 mod[:, CA, 0:B].unsqueeze(2).to_broadcast([P, B, D]), ALU.mult)\
                    .then_inc(wv_out_step, 1)

            def split_wfc():
                pool.wait_ge(ffn_loaded, 2 * 16)
                g_.tensor_copy(wfc_h[:, :], wfc_sb[:, :]).then_inc(wfc_step, 1)
                pool.wait_ge(wfc_step, 1)
                g_.tensor_tensor(wfc_l[:, :], wfc_sb[:, :], plain(wfc_h[:, :]), ALU.subtract)\
                    .then_inc(wfc_step, 1)

            def first_attention(b):
                split_wfc()
                add_bias_row(b, 0)
                add_bias_row(b, 1)
                scale_wv()
                split_z1_low(b, 0)
                deviation1(b + 1, 0)
                deviation1(b + 1, 1)
                split_z1_low(b, 1)
                deviation2(b, 0)
                h1_low_part(b + 1, 0)
                h1_low_part(b + 1, 1)
                h2_low_part(b, 0)

            def iteration(b, look_ahead=True):
                add_bias_row(b, 0)
                add_bias_row(b, 1)
                square(b, 0, 0)
                square(b, 0, 1)
                square(b, 0, 2)
                deviation2(b - 1, 1)
                square(b, 0, 3)
                split_z1_low(b, 0)
                if look_ahead:
                    deviation1(b + 1, 0)
                    deviation1(b + 1, 1)
                h2_low_part(b - 1, 1)
                square(b, 1, 0)
                square(b, 1, 1)
                split_z1_low(b, 1)
                square(b, 1, 2)
                square(b, 1, 3)
                deviation2(b, 0)
                if look_ahead:
                    h1_low_part(b + 1, 0)
                    h1_low_part(b + 1, 1)
                h2_low_part(b, 0)

            def last_feed_forward(b):
                deviation2(b - 1, 1)

            first_attention(0)
            iteration(1)
            with pool.Fori(2, B - 1) as b:
                iteration(b)
            iteration(B - 1, look_ahead=False)
            last_feed_forward(B)


def kernel(**inputs):
    import concourse.bacc as _bacc
    from concourse.bass_utils import run_bass_kernel_spmd as _run

    def get(name):
        return np.asarray(inputs[name])

    w_proj = get("L0_ffn_W_proj")
    d, f = w_proj.shape
    arrays = {
        "x": get("L0_attn_x"),
        "c_t": get("L0_c").T,
        "w_mod": get("L0_wmod"),
        "wq_t": get("L0_attn_Wq").T,
        "wk_t": get("L0_attn_Wk").T,
        "wv_t": get("L0_attn_Wv").T,
        "w_fc_t": get("L0_ffn_W_fc").T,
        "w_proj_t": w_proj.T.reshape(f // 128, 128, d).transpose(1, 0, 2),
        "bq": get("L0_attn_bq").reshape(-1, 1),
        "bk": get("L0_attn_bk").reshape(-1, 1),
        "bv": get("L0_attn_bv").reshape(-1, 1),
    }
    arrays = {k: np.ascontiguousarray(a) for k, a in arrays.items()}
    nc = _bacc.Bacc("TRN2", target_bir_lowering=False, num_devices=1)
    args = [nc.dram_tensor(k, a.shape, mybir.dt.from_np(a.dtype), kind="ExternalInput").ap()
            for k, a in arrays.items()]
    args.append(nc.dram_tensor("out", arrays["x"].shape, F32, kind="ExternalOutput").ap())
    build(nc, *args)
    return _run(nc, [arrays], core_ids=[0]).results[0]["out"]
```
